# Optimizing a Trainium2 kernel written in Bass

```python
import numpy as np
import jax
import jax.numpy as jnp

def _softmax(x, axis=-1):
    return jax.nn.softmax(x, axis=axis)

def _gelu(x):
    return jax.nn.gelu(x, approximate=True)

def _silu(x):
    return jax.nn.silu(x)

def _sigmoid(x):
    return jax.nn.sigmoid(x)

def _layernorm(x, axis=-1, eps=1e-05):
    m = jnp.mean(x, axis=axis, keepdims=True)
    v = jnp.var(x, axis=axis, keepdims=True)
    return (x - m) / jnp.sqrt(v + eps)

def _scatter_add(tgt, idx, src, axis=0):
    return tgt.at[idx].add(src)

def _segment_sum(src, seg, n):
    return jax.ops.segment_sum(src, seg, n)
kernel_name = 'mk_prb_d1_jaxref_r8_d59b60'

def setup_inputs(seed: int=0):
    np.random.seed(seed)
    _w = jnp.asarray

    def _L0_attn_setup():
        import jax, jax.numpy as jnp
        import numpy as np
        N_HEADS = 16
        ROPE_BASE = 10000.0

        def _rope_tables(seq_len, d_head, dtype):
            inv_freq = 1.0 / ROPE_BASE ** (jnp.arange(0, d_head, 2, dtype=jnp.float32) / d_head)
            t = jnp.arange(seq_len, dtype=jnp.float32)
            freqs = t[:, None] * inv_freq[None, :]
            return (jnp.cos(freqs).astype(dtype), jnp.sin(freqs).astype(dtype))

        def _apply_rope(x, cos, sin):
            half = x.shape[-1] // 2
            x1, x2 = (x[..., :half], x[..., half:])
            return jnp.concatenate([x1 * cos - x2 * sin, x2 * cos + x1 * sin], axis=-1)
        key = jax.random.key(seed)
        k1, k2, k3 = jax.random.split(key, 3)
        d_model = 128
        x = jax.random.normal(k1, (2, 256, d_model), dtype=jnp.float32)
        w_qkv = jax.random.normal(k2, (d_model, 3 * d_model), dtype=jnp.float32) * d_model ** (-0.5)
        w_out = jax.random.normal(k3, (d_model, d_model), dtype=jnp.float32) * d_model ** (-0.5)
        return {'x': x, 'w_qkv': w_qkv, 'w_out': w_out}
    _L0_attn_in = _L0_attn_setup()

    def _L0_ffn_setup():
        import jax, jax.numpy as jnp
        import numpy as np
        D_MODEL = 128
        D_FF = 512
        NUM_EXPERTS = 8
        B, N = (16, 128)
        key = jax.random.key(seed)
        ks = jax.random.split(key, 7)
        s_in = 1.0 / np.sqrt(D_MODEL)
        s_ff = 1.0 / np.sqrt(D_FF)
        return {'x': jax.random.normal(ks[0], (B, N, D_MODEL), dtype=jnp.float32), 'Wr': jax.random.uniform(ks[1], (D_MODEL, NUM_EXPERTS), jnp.float32, -s_in, s_in), 'br': jax.random.uniform(ks[2], (NUM_EXPERTS,), jnp.float32, -s_in, s_in), 'W1': jax.random.uniform(ks[3], (NUM_EXPERTS, D_MODEL, D_FF), jnp.float32, -s_in, s_in), 'b1': jax.random.uniform(ks[4], (NUM_EXPERTS, D_FF), jnp.float32, -s_in, s_in), 'W2': jax.random.uniform(ks[5], (NUM_EXPERTS, D_FF, D_MODEL), jnp.float32, -s_ff, s_ff), 'b2': jax.random.uniform(ks[6], (NUM_EXPERTS, D_MODEL), jnp.float32, -s_ff, s_ff)}
    _L0_ffn_in = _L0_ffn_setup()
    _d = {'L0_attn_x': _L0_attn_in['x'], 'L0_attn_w_qkv': _L0_attn_in['w_qkv'], 'L0_attn_w_out': _L0_attn_in['w_out'], 'L0_ffn_Wr': _L0_ffn_in['Wr'], 'L0_ffn_br': _L0_ffn_in['br'], 'L0_ffn_W1': _L0_ffn_in['W1'], 'L0_ffn_b1': _L0_ffn_in['b1'], 'L0_ffn_W2': _L0_ffn_in['W2'], 'L0_ffn_b2': _L0_ffn_in['b2']}
    _x0 = _d['L0_attn_x']
    _d['L0_attn_x'] = jax.random.normal(jax.random.fold_in(jax.random.key(seed), 1), (16, 512, 128), dtype=_x0.dtype)
    del _x0
    return _d

def reference(L0_attn_x, L0_attn_w_qkv, L0_attn_w_out, L0_ffn_Wr, L0_ffn_br, L0_ffn_W1, L0_ffn_b1, L0_ffn_W2, L0_ffn_b2):

    def _L0_attn_ref(x, w_qkv, w_out):
        import jax, jax.numpy as jnp
        import numpy as np
        N_HEADS = 16
        ROPE_BASE = 10000.0

        def _rope_tables(seq_len, d_head, dtype):
            inv_freq = 1.0 / ROPE_BASE ** (jnp.arange(0, d_head, 2, dtype=jnp.float32) / d_head)
            t = jnp.arange(seq_len, dtype=jnp.float32)
            freqs = t[:, None] * inv_freq[None, :]
            return (jnp.cos(freqs).astype(dtype), jnp.sin(freqs).astype(dtype))

        def _apply_rope(x, cos, sin):
            half = x.shape[-1] // 2
            x1, x2 = (x[..., :half], x[..., half:])
            return jnp.concatenate([x1 * cos - x2 * sin, x2 * cos + x1 * sin], axis=-1)
        B, S, D = x.shape
        H = N_HEADS
        dh = D // H
        scale = dh ** (-0.5)
        qkv = x @ w_qkv
        q, k, v = jnp.split(qkv, 3, axis=-1)

        def to_heads(t):
            return t.reshape(B, S, H, dh).transpose(0, 2, 1, 3)
        q, k, v = (to_heads(q), to_heads(k), to_heads(v))
        cos, sin = _rope_tables(S, dh, x.dtype)
        q = _apply_rope(q, cos, sin)
        k = _apply_rope(k, cos, sin)
        scores = jnp.einsum('bhqd,bhkd->bhqk', q, k) * scale
        causal = jnp.tril(jnp.ones((S, S), dtype=bool))
        scores = jnp.where(causal, scores, jnp.finfo(scores.dtype).min)
        attn = jax.nn.softmax(scores, axis=-1)
        out = jnp.einsum('bhqk,bhkd->bhqd', attn, v)
        out = out.transpose(0, 2, 1, 3).reshape(B, S, D)
        return out @ w_out

    def _L0_ffn_ref(x, Wr, br, W1, b1, W2, b2):
        import jax, jax.numpy as jnp
        import numpy as np
        D_MODEL = 128
        D_FF = 512
        NUM_EXPERTS = 8
        B, N = (16, 128)
        scores = jnp.einsum('bh,he->be', x.mean(axis=1), Wr) + br
        top1 = jnp.argmax(scores, axis=-1)
        w1 = W1[top1]
        c1 = b1[top1]
        w2 = W2[top1]
        c2 = b2[top1]
        h = jax.nn.relu(jnp.einsum('bnh,bhf->bnf', x, w1) + c1[:, None, :])
        out = jnp.einsum('bnf,bfh->bnh', h, w2) + c2[:, None, :]
        return out
    x = L0_attn_x
    xn = _layernorm(x, axis=-1)
    x = x + _L0_attn_ref(xn, L0_attn_w_qkv, L0_attn_w_out) + _L0_ffn_ref(xn, L0_ffn_Wr, L0_ffn_br, L0_ffn_W1, L0_ffn_b1, L0_ffn_W2, L0_ffn_b2)
    return x

_drawn_inputs = setup_inputs


def setup_inputs(seed=0):
    import zlib

    import numpy as np

    out = dict(_drawn_inputs(seed))
    spreads = {}
    factors = {'L0_ffn_b1': 3.023}
    for name, (base, spread) in spreads.items():
        noise = np.random.default_rng([zlib.crc32(name.encode()), seed]).standard_normal(out[name].shape)
        drawn = base * np.exp(spread * noise) if base else spread * noise
        out[name] = jnp.asarray(drawn.astype(out[name].dtype))
    for name, factor in factors.items():
        out[name] = (out[name] * factor).astype(out[name].dtype)
    return out
```

```python
import concourse.bass as bass
from concourse import mybir
from contextlib import ExitStack


def layernorm_attention_moe_kernel(
    nc: bass.Bass,
    x: bass.AP,
    w_qkv: bass.AP,
    w_out: bass.AP,
    Wr: bass.AP,
    br: bass.AP,
    W1: bass.AP,
    b1: bass.AP,
    W2: bass.AP,
    b2: bass.AP,
    ident_dram: bass.AP,
    cos_dram: bass.AP,
    sin_dram: bass.AP,
    k_rows_dram: bass.AP,
    q_rows_dram: bass.AP,
    zero_rows_dram: bass.AP,
    out: bass.AP,
):
    fp32 = mybir.dt.float32
    bf16 = mybir.dt.bfloat16
    u32 = mybir.dt.uint32
    ALU = mybir.AluOpType
    ACT = mybir.ActivationFunctionType
    AX = mybir.AxisListType

    B, S, D = x.shape
    E, _, F = W1.shape
    H = 16
    DH = D // H
    SCALE = float(DH) ** -0.5
    EPS = 1e-5
    TT = S // 128
    FC = F // 128
    KB = 64
    NBLK = S // KB
    PH = 4
    SLOTS = 18
    BANK = 512
    HALF_COLS = 2 * PH * S

    Q_PART = [0, 0, 0, 1, 1, 2]
    K_PART = [0, 1, 2, 0, 1, 0]
    NZ = len(Q_PART)
    M_ROW = NZ * DH
    K_OFF = 64
    K_DIAG = 128

    def pieces(chunk):
        if chunk < 4:
            return [(chunk, 0, 0), (chunk, 1, 512), (chunk, 7, 960)]
        if chunk < 8:
            return [(chunk - 4, 2, 0), (chunk - 4, 6, 384), (chunk - 4, 3, 512), (chunk - 4, 5, 832)]
        return [(p, 4, 256 * p) for p in range(PH)]

    PLACE = {(p, j): (c, col) for c in range(9) for p, j, col in pieces(c)}

    PV_PARTS = [([0, 7], 3), ([1], 3), ([2, 6], 7), ([3, 5, 4], 8)]
    PV_SLOT = {5: (0, 0, 0), 6: (0, 0, 1), 9: (0, 0, 2), 10: (0, 0, 3),
               14: (0, 1, 0), 15: (0, 1, 1), 0: (-1, 1, 2), 1: (-1, 1, 3)}

    CONSTS = 7 * 16
    N_PV = 8
    N_MAX = 2 * SLOTS

    def row(b, off):
        return 2 * b[0] + (b[1] + off) if isinstance(b, tuple) else b + off

    def at(n_per_row, b, off, j):
        if isinstance(b, tuple):
            return b[0] * (2 * n_per_row) + ((b[1] + off) * n_per_row + j + 1)
        return (b + off) * n_per_row + j + 1

    def later(value):
        return not isinstance(value, int) or value > 0

    def value(eng, v):
        return v if isinstance(v, int) else eng.to_reg(v)

    x_v = x.rearrange("b (t p) d -> b p t d", p=128)
    out_v = out.rearrange("b (t p) d -> b p t d", p=128)

    ctx = ExitStack()
    with ctx:
        def sb(name, shape, dt):
            return ctx.enter_context(nc.sbuf_tensor(name, shape, dt))

        def sem(name):
            return ctx.enter_context(nc.semaphore(name))

        q_stack = [sb(f"q_stack{i}", [128, H * S], bf16) for i in range(2)]
        k_stack = [sb(f"k_stack{i}", [128, H * S], bf16) for i in range(2)]
        probs = sb("probs", [128, 9, 1024], fp32)
        v_pad = [sb(f"v_pad{i}", [128, NBLK, 2 * PH, 32], fp32) for i in range(2)]
        x_in = sb("x_in", [128, TT, D], fp32)
        x_res = sb("x_res", [128, TT, D], fp32)
        out_sb = sb("out_sb", [128, TT, D], fp32)
        xn = sb("xn", [128, TT, D], fp32)
        xnT = [sb(f"xnT{i}", [128, S], fp32) for i in range(2)]
        x_sum = sb("x_sum", [128, 1], fp32)
        x_mean = sb("x_mean", [128, 1], fp32)
        stats = sb("stats", [128, TT, 6], fp32)
        mean_var = sb("mean_var", [128, TT, 2], fp32)
        var_eps = sb("var_eps", [128, TT], fp32)
        rstd = sb("rstd", [128, TT], fp32)
        minus_half = sb("minus_half", [128, TT], fp32)
        rope_a = sb("rope_a", [128, 2, S], fp32)
        rope_b = sb("rope_b", [128, 2, S], fp32)
        parts = sb("parts", [128, 2, 3, S], bf16)
        block_max = sb("block_max", [128, 2, 9, 16], fp32)
        row_max = sb("row_max", [128, 2, PH, NBLK], fp32)
        m_rest = sb("m_rest", [32, 128], fp32)
        m_parts = sb("m_parts", [32, 2, 3, 128], bf16)
        pv_sb = sb("pv_sb", [128, 2, S], fp32)
        numer = sb("numer", [128, S], fp32)
        denom = sb("denom", [128, S], fp32)
        attn = sb("attn", [128, S], fp32)
        zT = sb("zT", [128, S], fp32)
        hT = sb("hT", [128, FC, S], fp32)
        ffnT = [sb(f"ffnT{i}", [128, S], fp32) for i in range(2)]
        w1_sb = [sb(f"w1_sb{i}", [128, F], fp32) for i in range(2)]
        w2_sb = [sb(f"w2_sb{i}", [128, FC, D], fp32) for i in range(2)]
        b1_sb = [sb(f"b1_sb{i}", [128, FC], fp32) for i in range(2)]
        b2_sb = [sb(f"b2_sb{i}", [128, 1], fp32) for i in range(2)]
        wqkv_sb = sb("wqkv_sb", [128, 3 * D], fp32)
        w_rope = sb("w_rope", [128, 4, D], fp32)
        w_out_sb = sb("w_out_sb", [128, D], fp32)
        wr_sb = sb("wr_sb", [128, E], fp32)
        br_sb = sb("br_sb", [1, E], fp32)
        route = sb("route", [1, E], fp32)
        route_max = sb("route_max", [1, 8], fp32)
        route_idx = sb("route_idx", [1, 8], u32)
        ident = sb("ident", [128, 128], fp32)
        cosT = sb("cosT", [128, S], fp32)
        sinT = sb("sinT", [128, S], fp32)

        scores_ps = [ctx.enter_context(nc.psum_tensor(f"scores_ps{i}", [128, 2 * BANK], fp32)) for i in range(2)]
        max_ps = [ctx.enter_context(nc.psum_tensor(f"max_ps{i}", [128, BANK], fp32)) for i in range(2)]
        pv_ps = ctx.enter_context(nc.psum_tensor("pv_ps", [128, BANK], fp32))
        misc_ps = ctx.enter_context(nc.psum_tensor("misc_ps", [128, BANK], fp32))

        const_loaded = sem("const_loaded")
        stack_const = sem("stack_const")
        w_ready = sem("w_ready")
        pad_ready = sem("pad_ready")
        half_ready = sem("half_ready")
        x_loaded = sem("x_loaded")
        res_loaded = sem("res_loaded")
        stats_done = sem("stats_done")
        aggr_done = sem("aggr_done")
        var_done = sem("var_done")
        rstd_done = sem("rstd_done")
        xn_done = sem("xn_done")
        xnT_ps_done = sem("xnT_ps_done")
        xnT_done = sem("xnT_done")
        mean_done = sem("mean_done")
        route_ps_done = sem("route_ps_done")
        route_done = sem("route_done")
        top_done = sem("top_done")
        expert_done = sem("expert_done")
        expert_loaded = sem("expert_loaded")
        proj_done = sem("proj_done")
        rope_done = sem("rope_done")
        rotated = sem("rotated")
        part0_done = sem("part0_done")
        rest_done = sem("rest_done")
        part1_done = sem("part1_done")
        part2_done = sem("part2_done")
        stack_loaded = [sem(f"stack_loaded{h}") for h in range(2)]
        max_mm_done = sem("max_mm_done")
        block_max_done = sem("block_max_done")
        row_max_done = sem("row_max_done")
        maxT_done = sem("maxT_done")
        m_split = sem("m_split")
        m_rows_loaded = [sem(f"m_rows_loaded{h}") for h in range(2)]
        scores_done = sem("scores_done")
        exp_done = sem("exp_done")
        v_ps_done = sem("v_ps_done")
        v_done = sem("v_done")
        pv_done = sem("pv_done")
        pv_copied = sem("pv_copied")
        gathered = [sem(f"gathered{h}") for h in range(2)]
        recip_done = sem("recip_done")
        attn_done = sem("attn_done")
        proj_out_done = sem("proj_out_done")
        z_done = sem("z_done")
        zT_done = sem("zT_done")
        out_done = sem("out_done")
        ffn1_done = sem("ffn1_done")
        relu_done = sem("relu_done")
        ffn2_done = sem("ffn2_done")
        ffn_done = sem("ffn_done")
        stored = sem("stored")

        block = ctx.enter_context(nc.Block())

        def rows(eng, step):
            for b in range(-3, 1):
                step(b, b % 2, lambda off, b=b: 0 <= b + off < B)
            with eng.Fori(0, (B - 4) // 2) as i:
                step((i, 1), 1, lambda off: True)
                step((i, 2), 0, lambda off: True)
            for b in range(B - 3, B + 1):
                step(b, b % 2, lambda off, b=b: 0 <= b + off < B)

        @block.sync
        def _(sp):
            sp.dma_start(wqkv_sb[:, :], w_qkv).then_inc(const_loaded, 16)
            sp.dma_start(ident[:, :], ident_dram).then_inc(const_loaded, 16)
            sp.dma_start(wr_sb[:, :], Wr).then_inc(const_loaded, 16)
            sp.dma_start(br_sb[:, :], br.rearrange("(a e) -> a e", a=1)).then_inc(const_loaded, 16)
            sp.dma_start(cosT[:, :], cos_dram).then_inc(const_loaded, 16)
            sp.dma_start(sinT[:, :], sin_dram).then_inc(const_loaded, 16)
            sp.dma_start(w_out_sb[:, :], w_out).then_inc(const_loaded, 16)

            def stack_constants(i):
                nq, nk = q_rows_dram.shape[0], k_rows_dram.shape[0]
                sp.dma_start(q_stack[i][128 - nq:128, :].rearrange("p (h n) -> p h n", n=S),
                             q_rows_dram.unsqueeze(1).to_broadcast([nq, H, S])).then_inc(stack_const, 16)
                sp.dma_start(k_stack[i][128 - nk:128, :].rearrange("p (h n) -> p h n", n=S),
                             k_rows_dram.unsqueeze(1).to_broadcast([nk, H, S])).then_inc(stack_const, 16)

            def load_stack(b, off, half, par):
                cols = slice(half * HALF_COLS, (half + 1) * HALF_COLS)
                dst_rows = slice(64 * half, 64 * half + 64)
                for qk, stack, part in ((0, q_stack[par], Q_PART), (1, k_stack[par], K_PART)):
                    for z in range(NZ):
                        sp.dma_start(stack[DH * z:DH * z + DH, cols].rearrange("p (s n) -> p s n", n=S),
                                     parts[dst_rows, qk, part[z], :]).then_inc(stack_loaded[half], 16)
                sp.dma_start(q_stack[par][M_ROW:M_ROW + 3, cols], zero_rows_dram).then_inc(stack_loaded[half], 16)

            def load_m_rows(b, off, half, par):
                for part in range(3):
                    for r in range(2):
                        first = (half * 8 + r * PH) * S
                        sp.dma_start(q_stack[par][M_ROW + part:M_ROW + part + 1, first:first + PH * S]
                                     .rearrange("p (g q) -> p g q", q=KB),
                                     m_parts[:, half, part, KB * r:KB * r + KB]).then_inc(m_rows_loaded[half], 16)

            def gather(half):
                for c in range(PH):
                    at_row = 64 * half + 16 * c
                    sp.dma_start(numer[at_row:at_row + 16, :], pv_sb[32 * c:32 * c + 16, half, :])\
                      .then_inc(gathered[half], 16)
                    sp.dma_start(denom[at_row:at_row + 16, :], pv_sb[32 * c + 16:32 * c + 32, half, :])\
                      .then_inc(gathered[half], 16)

            def step(b, par, has):
                if has(1):
                    first, second = value(sp, at(2, b, 1, 1)), value(sp, at(SLOTS, b, -1, 17))
                    sp.wait_ge(part2_done, first)
                    if later(v := second):
                        sp.wait_ge(scores_done, v)
                    load_stack(b, 1, 1, 1 - par)
                if has(3):
                    if later(v := at(TT, b, 2, TT - 1)):
                        sp.wait_ge(xn_done, v)
                    sp.dma_start(x_in[:, :, :], x_v[row(b, 3), :, :, :]).then_inc(x_loaded, 16)
                if has(0):
                    sp.wait_ge(m_split, at(8, b, 0, 7))
                    load_m_rows(b, 0, 1, par)
                if has(-1):
                    sp.wait_ge(pv_copied, at(2, b, -1, 1))
                    gather(1)
                if has(2):
                    first, second = value(sp, at(1, b, 0, 0)), value(sp, at(1, b, 2, 0))
                    sp.wait_ge(const_loaded, CONSTS)
                    if later(v := first):
                        sp.wait_ge(ffn2_done, v)
                    sp.wait_ge(expert_done, second)
                    e = sp.value_load(route_idx[0:1, 0:1], min_val=0, max_val=E - 1)
                    sp.dma_start(w1_sb[par][:, :], W1[e, :, :]).then_inc(expert_loaded, 16)
                    sp.dma_start(w2_sb[par][:, :, :], W2[e, :, :].rearrange("(c p) d -> p c d", p=128))\
                      .then_inc(expert_loaded, 16)
                    with nc.allow_non_contiguous_dma(reason="a bias value per partition"):
                        sp.dma_start(b1_sb[par][:, :], b1[e, :].rearrange("(c p) -> p c", p=128))\
                          .then_inc(expert_loaded, 16)
                        sp.dma_start(b2_sb[par][:, :], b2[e, :].rearrange("(p c) -> p c", c=1))\
                          .then_inc(expert_loaded, 16)
                if has(-1):
                    sp.wait_ge(out_done, at(1, b, -1, 0))
                    sp.dma_start(out_v[row(b, -1), :, :, :], out_sb[:, :, :]).then_inc(stored, 16)
                if has(2):
                    if isinstance(b, int) and b < 0:
                        stack_constants(par)
                    first, second = value(sp, at(2, b, 2, 1)), value(sp, at(SLOTS, b, 0, 8))
                    sp.wait_ge(part2_done, first)
                    if later(v := second):
                        sp.wait_ge(scores_done, v)
                    load_stack(b, 2, 0, par)
                if has(0):
                    first, second = value(sp, at(1, b, -1, 0)), value(sp, at(2, b, 0, 0))
                    if later(v := first):
                        sp.wait_ge(attn_done, v)
                    sp.wait_ge(pv_copied, second)
                    gather(0)
                if has(1):
                    sp.wait_ge(m_split, at(8, b, 1, 3))
                    load_m_rows(b, 1, 0, 1 - par)
                if has(0):
                    if later(v := at(16, b, -1, 15)):
                        sp.wait_ge(stored, v)
                    sp.dma_start(x_res[:, :, :], x_v[row(b, 0), :, :, :]).then_inc(res_loaded, 16)

            rows(sp, step)
            sp.wait_ge(stored, 16 * B)

        @block.gpsimd
        def _(pool):
            pool.memset(minus_half[:, :], -0.5).then_inc(half_ready, 1)
            pool.wait_ge(half_ready, 1)
            pads = [(0, 8, 0.0), (64, 0, 0.0), (0, 16, 1.0), (64, 16, 0.0), (0, 24, 0.0), (64, 24, 1.0)]
            for n in range(12):
                first, col, fill = pads[n % 6]
                if later(v := n):
                    pool.wait_ge(pad_ready, v)
                pool.memset(v_pad[n // 6][first:first + 64, :, :, col:col + 8], fill).then_inc(pad_ready, 1)
            pool.wait_ge(pad_ready, 12)

            def step(b, par, has):
                if has(2):
                    def rotate(qk):
                        pool.wait_ge(rope_done, at(4, b, 2, 2 * qk + 1))
                        pool.tensor_tensor(rope_a[:, qk, :], rope_a[:, qk, :], rope_b[:, qk, :], ALU.add)\
                            .then_inc(rotated, 1)

                    def rest(qk):
                        pool.wait_ge(part0_done, at(2, b, 2, qk))
                        pool.tensor_tensor(rope_b[:, qk, :], rope_a[:, qk, :], parts[:, qk, 0, :], ALU.subtract)\
                            .then_inc(rest_done, 1)

                    def last_part(qk):
                        pool.wait_ge(part1_done, at(2, b, 2, qk))
                        pool.tensor_tensor(parts[:, qk, 2, :], rope_b[:, qk, :], parts[:, qk, 1, :], ALU.subtract)\
                            .then_inc(part2_done, 1)

                    rotate(0)
                    rest(0)
                    rotate(1)
                    last_part(0)
                    rest(1)
                    last_part(1)
                if has(3):
                    pool.wait_ge(var_done, at(1, b, 3, 0))
                    pool.tensor_tensor(rstd[:, :], var_eps[:, :], minus_half[:, :], ALU.pow).then_inc(rstd_done, 1)

            rows(pool, step)

        @block.scalar
        def _(act):
            act.wait_ge(pad_ready, 12)

            def exp(b, k):
                act.wait_ge(scores_done, at(SLOTS, b, 0, k))
                last = 1 if k % 9 < 4 else 3
                if later(v := at(N_PV, b, 0, last) if k >= 9 else at(N_PV, b, -1, 4 + last)):
                    act.wait_ge(pv_done, v)
                nc.scalar.activation(probs[:, k % 9, :], scores_ps[k % 2][:, :], ACT.Exp, scale=SCALE)\
                  .then_inc(exp_done, 1)

            def copy_pv(b, off, half):
                act.wait_ge(pv_done, at(N_PV, b, off, 4 * half + 3))
                nc.scalar.activation(pv_sb[:, half, :], pv_ps[:, :], ACT.Copy).then_inc(pv_copied, 1)

            def relu(b, par, c):
                act.wait_ge(ffn1_done, at(FC, b, 1, c))
                nc.scalar.activation(hT[:, c, :], misc_ps[:, :], ACT.Relu, bias=b1_sb[1 - par][:, c:c + 1])\
                  .then_inc(relu_done, 1)

            def part(b, qk, i):
                src = rope_a if i == 0 else rope_b
                act.wait_ge(rotated if i == 0 else rest_done, at(2, b, 2, qk))
                if i == 0 and qk == 0:
                    for half in range(2):
                        if later(v := at(208, b, 1, 207)):
                            act.wait_ge(stack_loaded[half], v)
                nc.scalar.activation(parts[:, qk, i, :], src[:, qk, :], ACT.Copy)\
                  .then_inc(part0_done if i == 0 else part1_done, 1)

            def step(b, par, has):
                for k in range(SLOTS):
                    if has(0):
                        exp(b, k)
                    if k == 0 and has(2):
                        if later(v := at(1, b, 1, 0)):
                            act.wait_ge(mean_done, v)
                        act.wait_ge(xnT_ps_done, at(1, b, 2, 0))
                        nc.scalar.activation(xnT[par][:, :], misc_ps[:, :], ACT.Identity, accum_out=x_sum[:, :])\
                          .then_inc(xnT_done, 1)
                    if k == 2 and has(-1):
                        copy_pv(b, -1, 1)
                    if k == 3 and has(1):
                        act.wait_ge(v_ps_done, at(1, b, 1, 0))
                        for r in range(2):
                            nc.scalar.activation(
                                v_pad[1 - par][64 * r:64 * r + 64, :, :, 8 * r:8 * r + 8],
                                misc_ps[64 * r:64 * r + 64, :].rearrange("k (j p d) -> k j p d", j=NBLK, d=DH),
                                ACT.Copy).then_inc(v_done, 1)
                    if k == 7 and has(2):
                        part(b, 0, 0)
                    if k == 9 and has(2):
                        part(b, 0, 1)
                        part(b, 1, 0)
                    if k in (9, 12, 13, 14) and has(1):
                        relu(b, par, [9, 12, 13, 14].index(k))
                    if k == 11 and has(0):
                        copy_pv(b, 0, 0)
                    if k == 11 and has(2):
                        part(b, 1, 1)
                    if k == 15 and has(1):
                        if later(v := at(1, b, -1, 0)):
                            act.wait_ge(z_done, v)
                        act.wait_ge(ffn2_done, at(1, b, 1, 0))
                        nc.scalar.activation(ffnT[1 - par][:, :], misc_ps[:, :], ACT.Identity,
                                             bias=b2_sb[1 - par][:, 0:1]).then_inc(ffn_done, 1)

            rows(act, step)

        @block.tensor
        def _(pe):
            pe.wait_ge(const_loaded, CONSTS)
            pe.wait_ge(w_ready, 12)

            def slot_cols(half, r, p):
                return (half * 8 + r * PH + p) * S

            def block_pair(ps, base, half, p, j, col, stat, mov, transposed):
                i = j if transposed else NBLK - 1 - j
                n = S - KB * j - KB
                diag = col - base if transposed else col - base + n
                rest = col - base + KB if transposed else col - base
                rest_at = KB * (i + 1) if transposed else 0
                for r in range(2):
                    c = slot_cols(half, r, p) + KB * i
                    last = nc.tensor.matmul(ps[64 * r:64 * r + 64, diag:diag + KB], stat[0:K_DIAG, c:c + KB],
                                            mov[0:K_DIAG, c:c + KB], start=True, stop=True)
                for r in range(2 if n else 0):
                    c = slot_cols(half, r, p)
                    last = nc.tensor.matmul(ps[64 * r:64 * r + 64, rest:rest + n],
                                            stat[0:K_OFF, c + KB * i:c + KB * i + KB],
                                            mov[0:K_OFF, c + rest_at:c + rest_at + n], start=True, stop=True)
                return last

            def scores(b, par, k):
                if k % 9 == 0:
                    pe.wait_ge(m_rows_loaded[k // 9], at(96, b, 0, 95))
                if later(v := at(SLOTS, b, 0, k - 2)):
                    pe.wait_ge(exp_done, v)
                for p, j, col in pieces(k % 9):
                    last = block_pair(scores_ps[k % 2], 0, k // 9, p, j, col, k_stack[par], q_stack[par], True)
                last.then_inc(scores_done, 1)

            def max_scores(b, par, k):
                if k % 9 == 0:
                    pe.wait_ge(stack_loaded[k // 9], at(208, b, 1, 207))
                    pe.wait_ge(stack_const, 32 if b == -1 else 64)
                for bank in range(2):
                    if later(v := at(N_MAX, b, 1, 2 * k + bank - 2)):
                        pe.wait_ge(block_max_done, v)
                    for p, j, col in pieces(k % 9):
                        if col // BANK == bank:
                            last = block_pair(max_ps[bank], bank * BANK, k // 9, p, j, col,
                                              q_stack[1 - par], k_stack[1 - par], False)
                    last.then_inc(max_mm_done, 1)

            def pv(b, off, par, half, i):
                blocks, chunk = PV_PARTS[i]
                if i == 0:
                    pe.wait_ge(v_done, at(2, b, off, 1))
                    if later(v := at(2, b, off, half - 1)):
                        pe.wait_ge(pv_copied, v)
                pe.wait_ge(exp_done, at(SLOTS, b, off, 9 * half + chunk))
                for j in blocks:
                    for p in range(PH):
                        ch, col = PLACE[p, j]
                        last = nc.tensor.matmul(pv_ps[32 * p:32 * p + 32, KB * j:S],
                                                v_pad[par][:, j, PH * half + p, :],
                                                probs[:, ch, col:col + S - KB * j],
                                                start=(j == 0), stop=(j == 4), skip_group_check=True)
                last.then_inc(pv_done, 1)

            def transpose_max(b, off, half):
                pe.wait_ge(row_max_done, at(16, b, off, 8 * half + 7))
                nc.tensor.transpose(misc_ps[0:32, 0:128], row_max[:, half, :, :].rearrange("q p i -> q (p i)"),
                                    ident[:, :]).then_inc(maxT_done, 1)

            def project(b, par, i):
                nc.tensor.matmul(misc_ps[:, :], w_rope[:, i, :], xnT[par][:, :], start=True, stop=True)\
                  .then_inc(proj_done, 1)

            def misc(b, par, k, has):
                if k == 0 and has(2):
                    if later(v := at(1, b, 0, 0)):
                        pe.wait_ge(ffn_done, v)
                    pe.wait_ge(xn_done, at(TT, b, 2, TT - 1))
                    for t in range(TT):
                        last = nc.tensor.transpose(misc_ps[:, 128 * t:128 * t + 128], xn[:, t, :], ident[:, :])
                    last.then_inc(xnT_ps_done, 1)
                if k == 1 and has(2):
                    pe.wait_ge(xnT_done, at(1, b, 2, 0))
                    pe.wait_ge(mean_done, at(1, b, 2, 0))
                    nc.tensor.matmul(misc_ps[0:1, 0:E], x_mean[:, :], wr_sb[:, :], start=True, stop=True)\
                      .then_inc(route_ps_done, 1)
                if k == 2 and has(0):
                    if later(v := at(1, b, 0, 0)):
                        pe.wait_ge(ffn_done, v)
                    pe.wait_ge(route_done, at(1, b, 2, 0) if has(2) else B)
                    transpose_max(b, 0, 1)
                if k == 3 and has(1):
                    pe.wait_ge(route_done, at(1, b, 2, 0) if has(2) else B)
                    if later(v := at(8, b, 0, 5)):
                        pe.wait_ge(m_split, v)
                    for j in range(NBLK):
                        for r in range(2):
                            last = nc.tensor.matmul(
                                misc_ps[64 * r:64 * r + 64, KB * j:KB * j + KB],
                                xnT[1 - par][:, KB * j:KB * j + KB],
                                wqkv_sb[:, 2 * D:3 * D].rearrange("k (p r d) -> k p r d", r=2, d=DH)[:, :, r, :],
                                start=True, stop=True)
                    last.then_inc(v_ps_done, 1)
                if 4 <= k < 8 and has(2):
                    i = k - 4
                    if i == 0:
                        if later(v := at(2, b, 1, 1)):
                            pe.wait_ge(v_done, v)
                        pe.wait_ge(route_done, at(1, b, 2, 0))
                    if later(v := at(4, b, 2, i - 1)):
                        pe.wait_ge(rope_done, v)
                    project(b, par, i)
                if k == 8 and has(-1):
                    if has(0):
                        if later(v := at(8, b, 0, 5)):
                            pe.wait_ge(m_split, v)
                    if has(1):
                        if later(v := at(2, b, 1, 1)):
                            pe.wait_ge(v_done, v)
                    pe.wait_ge(rope_done, at(4, b, 2, 3) if has(2) else 4 * B)
                    pe.wait_ge(attn_done, at(1, b, -1, 0))
                    nc.tensor.matmul(misc_ps[:, :], w_out_sb[:, :], attn[:, :], start=True, stop=True)\
                      .then_inc(proj_out_done, 1)
                if k in (9, 12, 13, 14) and has(1):
                    c = [9, 12, 13, 14].index(k)
                    if c == 0:
                        if later(v := at(1, b, -1, 0)):
                            pe.wait_ge(z_done, v)
                        pe.wait_ge(rope_done, at(4, b, 2, 3) if has(2) else 4 * B)
                        pe.wait_ge(expert_loaded, at(64, b, 1, 63))
                        if later(v := at(2, b, 1, 1)):
                            pe.wait_ge(v_done, v)
                    if c == 1:
                        pe.wait_ge(m_split, at(8, b, 1, 1))
                    if later(v := at(FC, b, 1, c - 1)):
                        pe.wait_ge(relu_done, v)
                    nc.tensor.matmul(misc_ps[:, :], w1_sb[1 - par][:, 128 * c:128 * c + 128], xnT[1 - par][:, :],
                                     start=True, stop=True).then_inc(ffn1_done, 1)
                if k == 10 and has(-1):
                    if has(1):
                        pe.wait_ge(relu_done, at(FC, b, 1, 0))
                    if later(v := at(1, b, -1, 0)):
                        pe.wait_ge(z_done, v)
                    for t in range(TT):
                        last = nc.tensor.transpose(misc_ps[:, 128 * t:128 * t + 128],
                                                   zT[:, 128 * t:128 * t + 128], ident[:, :])
                    last.then_inc(zT_done, 1)
                if k == 11 and has(1):
                    if later(v := at(1, b, -1, 0)):
                        pe.wait_ge(out_done, v)
                    pe.wait_ge(relu_done, at(FC, b, 1, 0))
                    transpose_max(b, 1, 0)
                if k == 15 and has(1):
                    pe.wait_ge(relu_done, at(FC, b, 1, FC - 1))
                    for c in range(FC):
                        last = nc.tensor.matmul(misc_ps[:, :], w2_sb[1 - par][:, c, :], hT[:, c, :],
                                                start=(c == 0), stop=(c == FC - 1))
                    last.then_inc(ffn2_done, 1)

            def step(b, par, has):
                for k in range(SLOTS):
                    if has(0):
                        scores(b, par, k)
                    if k in PV_SLOT and has(PV_SLOT[k][0]):
                        off, half, i = PV_SLOT[k]
                        pv(b, off, par if off == 0 else 1 - par, half, i)
                    if has(1):
                        max_scores(b, par, k)
                    misc(b, par, k, has)

            rows(pe, step)

        @block.vector
        def _(dve):
            dve.wait_ge(const_loaded, CONSTS)
            for qk in range(2):
                for half in range(2):
                    src = wqkv_sb[:, qk * D + 64 * half:qk * D + 64 * half + 64]\
                        .rearrange("k (p r d) -> k d r p", r=2, d=DH)
                    plain, swapped = (w_rope[:, 2 * qk + i, 64 * half:64 * half + 64]
                                      .rearrange("k (d r p) -> k d r p", r=2, d=DH) for i in range(2))
                    nc.vector.tensor_copy(plain, src).then_inc(w_ready, 1)
                    nc.vector.tensor_copy(swapped[:, 0:4, :, :], src[:, 4:8, :, :]).then_inc(w_ready, 1)
                    nc.vector.tensor_copy(swapped[:, 4:8, :, :], src[:, 0:4, :, :]).then_inc(w_ready, 1)

            def block_maxima(b, k):
                for bank in range(2):
                    dve.wait_ge(max_mm_done, at(N_MAX, b, 1, 2 * k + bank))
                    nc.vector.tensor_reduce(block_max[:, k // 9, k % 9, 8 * bank:8 * bank + 8],
                                            max_ps[bank][:, :].rearrange("q (a c) -> q a c", c=KB),
                                            AX.X, ALU.max).then_inc(block_max_done, 1)

            def row_maxima(b, off, half):
                dve.wait_ge(block_max_done, at(N_MAX, b, off, 18 * half + 17))
                for j in range(NBLK):
                    chunk, col = PLACE[0, j]
                    n, a = NBLK - j, col // KB
                    if chunk == 8:
                        src = block_max[:, half, 8, :].rearrange("q (p a) -> q p a", p=PH)
                    else:
                        src = block_max[:, half, chunk:chunk + PH, a:a + n]
                    nc.vector.tensor_reduce(row_max[:, half, :, NBLK - 1 - j], src, AX.X, ALU.max)\
                      .then_inc(row_max_done, 1)

            def split_max(b, off, half):
                mT = misc_ps[0:32, 0:128]
                if later(v := at(96, b, off - 1, 95)):
                    dve.wait_ge(m_rows_loaded[half], v)
                dve.wait_ge(maxT_done, at(2, b, off, half))
                nc.vector.tensor_scalar(m_parts[:, half, 0, :], mT, -1.0, None, ALU.mult).then_inc(m_split, 1)
                dve.wait_ge(m_split, at(8, b, off, 4 * half))
                nc.vector.scalar_tensor_tensor(out=m_rest[:, :], in0=mT, scalar=-1.0, in1=m_parts[:, half, 0, :],
                                               op0=ALU.mult, op1=ALU.subtract).then_inc(m_split, 1)
                dve.wait_ge(m_split, at(8, b, off, 4 * half + 1))
                nc.vector.tensor_copy(m_parts[:, half, 1, :], m_rest[:, :]).then_inc(m_split, 1)
                dve.wait_ge(m_split, at(8, b, off, 4 * half + 2))
                nc.vector.tensor_tensor(m_parts[:, half, 2, :], m_rest[:, :], m_parts[:, half, 1, :],
                                        ALU.subtract).then_inc(m_split, 1)

            def rope(b, i):
                dve.wait_ge(proj_done, at(4, b, 2, i))
                dst, table = ((rope_a, cosT), (rope_b, sinT))[i % 2]
                if i % 2:
                    if later(v := at(2, b, 1, i // 2)):
                        dve.wait_ge(part2_done, v)
                nc.vector.tensor_tensor(dst[:, i // 2, :], misc_ps[:, :], table[:, :], ALU.mult)\
                  .then_inc(rope_done, 1)

            def router(b):
                dve.wait_ge(route_ps_done, at(1, b, 2, 0))
                nc.vector.tensor_tensor(route[:, :], misc_ps[0:1, 0:E], br_sb[:, :], ALU.add)\
                  .then_inc(route_done, 1)
                done = value(dve, at(1, b, 2, 0))
                dve.wait_ge(const_loaded, CONSTS)
                dve.wait_ge(route_done, done)
                nc.vector.max(route_max[:, :], route[:, :]).then_inc(top_done, 1)
                loaded = value(dve, at(64, b, 1, 63))
                dve.wait_ge(const_loaded, CONSTS)
                dve.wait_ge(top_done, done)
                if later(v := loaded):
                    dve.wait_ge(expert_loaded, v)
                nc.vector.max_index(route_idx[:, :], route_max[:, :], route[:, :]).then_inc(expert_done, 1)

            def normalise(b):
                for half in range(2):
                    dve.wait_ge(gathered[half], at(128, b, -1, 127))
                nc.vector.reciprocal(denom[:, :], denom[:, :]).then_inc(recip_done, 1)
                dve.wait_ge(recip_done, at(1, b, -1, 0))
                nc.vector.tensor_tensor(attn[:, :], numer[:, :], denom[:, :], ALU.mult).then_inc(attn_done, 1)

            def ln_stats(b):
                dve.wait_ge(x_loaded, at(16, b, 3, 15))
                for t in range(TT):
                    nc.vector.bn_stats(stats[:, t, :], x_in[:, t, :]).then_inc(stats_done, 1)
                for t in range(TT):
                    done = value(dve, at(TT, b, 3, t))
                    dve.wait_ge(const_loaded, CONSTS)
                    dve.wait_ge(stats_done, done)
                    nc.vector.bn_aggr(mean_var[:, t, :], stats[:, t, :]).then_inc(aggr_done, 1)
                dve.wait_ge(aggr_done, at(TT, b, 3, TT - 1))
                nc.vector.tensor_scalar(var_eps[:, :], mean_var[:, :, 1], EPS, None, ALU.add).then_inc(var_done, 1)

            def ln_apply(b):
                dve.wait_ge(rstd_done, at(1, b, 3, 0))
                if later(v := at(1, b, 2, 0)):
                    dve.wait_ge(xnT_ps_done, v)
                for t in range(TT):
                    nc.vector.tensor_scalar(xn[:, t, :], x_in[:, t, :], mean_var[:, t, 0:1], rstd[:, t:t + 1],
                                            ALU.subtract, ALU.mult).then_inc(xn_done, 1)

            def step(b, par, has):
                for k in range(SLOTS):
                    if k == 0 and has(0):
                        row_maxima(b, 0, 1)
                    if k == 0 and has(2):
                        dve.wait_ge(xnT_done, at(1, b, 2, 0))
                        nc.vector.tensor_scalar(x_mean[:, :], x_sum[:, :], 1.0 / S, None, ALU.mult)\
                          .then_inc(mean_done, 1)
                    if has(1):
                        block_maxima(b, k)
                    if k == 1 and has(2):
                        router(b)
                    if k == 2 and has(0):
                        split_max(b, 0, 1)
                    if 4 <= k < 8 and has(2):
                        rope(b, k - 4)
                    if k == 6 and has(-1):
                        normalise(b)
                    if k == 8 and has(-1):
                        dve.wait_ge(proj_out_done, at(1, b, -1, 0))
                        dve.wait_ge(ffn_done, at(1, b, -1, 0))
                        nc.vector.tensor_tensor(zT[:, :], misc_ps[:, :], ffnT[1 - par][:, :], ALU.add)\
                          .then_inc(z_done, 1)
                    if k == 9 and has(1):
                        row_maxima(b, 1, 0)
                    if k == 10 and has(-1):
                        dve.wait_ge(zT_done, at(1, b, -1, 0))
                        dve.wait_ge(res_loaded, at(16, b, -1, 15))
                        nc.vector.tensor_tensor(out_sb[:, :, :], misc_ps[:, :].rearrange("p (t d) -> p t d", d=D),
                                                x_res[:, :, :], ALU.add).then_inc(out_done, 1)
                    if k == 11 and has(1):
                        split_max(b, 1, 0)
                    if k == 12 and has(3):
                        ln_stats(b)
                    if k == 15 and has(3):
                        ln_apply(b)

            rows(dve, step)


_INS = ['L0_attn_x', 'L0_attn_w_qkv', 'L0_attn_w_out', 'L0_ffn_Wr', 'L0_ffn_br', 'L0_ffn_W1', 'L0_ffn_b1',
        'L0_ffn_W2', 'L0_ffn_b2']
_OUTS = [((16, 512, 128), 'float32')]


def _constants():
    import numpy as np
    from concourse import mybir
    bf16 = mybir.dt.np(mybir.dt.bfloat16)
    S, DH, KB, MASKED = 512, 8, 64, -1e30
    ident = np.eye(128, dtype=np.float32)
    inv_freq = (1.0 / np.float32(10000.0) ** (np.arange(0, DH, 2, dtype=np.float32) / DH)).astype(np.float32)
    freqs = np.arange(S, dtype=np.float32)[:, None] * inv_freq[None, :]
    cos, sin = np.cos(freqs).astype(np.float32), np.sin(freqs).astype(np.float32)
    d = (np.arange(128) % 64) // 8
    cosT = np.ascontiguousarray(cos[:, d % 4].T)
    sinT = np.ascontiguousarray(sin[:, d % 4].T * np.where(d < 4, -1, 1)[:, None].astype(np.float32))
    col = np.arange(S) % KB
    row = np.arange(KB)
    k_rows = np.zeros((80, S), np.float32)
    k_rows[0:3] = 1.0
    k_rows[16:80] = np.where(col[None, :] > row[:, None], MASKED, 0.0)
    q_rows = np.zeros((77, S), np.float32)
    q_rows[13:77] = col[None, :] == row[:, None]
    return {"ident": ident, "cos": cosT, "sin": sinT, "k_rows": k_rows.astype(bf16),
            "q_rows": q_rows.astype(bf16), "zero_rows": np.zeros((3, 8 * S), bf16)}


def kernel(**inputs):
    import numpy as _np
    import concourse.bacc as _bacc
    from concourse import mybir as _mybir
    from concourse.bass_utils import run_bass_kernel_spmd as _run

    nc = _bacc.Bacc("TRN2", target_bir_lowering=False, num_devices=1)
    arrays, args = {}, []
    named = {name: inputs[name] for name in _INS} | _constants()
    for name, a in named.items():
        a = _np.ascontiguousarray(a)
        arrays[f"in_{name}_dram"] = a
        args.append(nc.dram_tensor(f"in_{name}_dram", a.shape, _mybir.dt.from_np(a.dtype), kind="ExternalInput").ap())
    for i, (shape, dtype) in enumerate(_OUTS):
        dt = _mybir.dt.from_np(_np.dtype(dtype))
        args.append(nc.dram_tensor(f"out_{i}_dram", shape, dt, kind="ExternalOutput").ap())
    layernorm_attention_moe_kernel(nc, *args)
    r = _run(nc, [arrays], core_ids=[0])
    got = tuple(r.results[0][f"out_{i}_dram"] for i in range(len(_OUTS)))
    return got[0]
```

```python
import concourse.bass as bass
from concourse import mybir
from contextlib import ExitStack


def layernorm_attention_moe_kernel(
    nc: bass.Bass,
    x: bass.AP,
    w_qkv: bass.AP,
    w_out: bass.AP,
    Wr: bass.AP,
    br: bass.AP,
    W1: bass.AP,
    b1: bass.AP,
    W2: bass.AP,
    b2: bass.AP,
    ident_dram: bass.AP,
    cos_dram: bass.AP,
    sin_dram: bass.AP,
    mask_dram: bass.AP,
    ones_dram: bass.AP,
    zeros_dram: bass.AP,
    q_parts_dram: bass.AP,
    k_parts_dram: bass.AP,
    pv_dram: bass.AP,
    out: bass.AP,
):
    fp32 = mybir.dt.float32
    bf16 = mybir.dt.bfloat16
    u32 = mybir.dt.uint32
    ALU = mybir.AluOpType
    ACT = mybir.ActivationFunctionType
    AX = mybir.AxisListType

    B, S, D = x.shape
    E, _, F = W1.shape
    H = 16
    DH = D // H
    SCALE = float(DH) ** -0.5
    EPS = 1e-5
    TT = S // 128
    FC = F // 128
    KB = 64
    NBLK = S // KB
    PH = 4
    SLOTS = 18
    BANK = 512
    HALF_COLS = 2 * PH * S

    Q_PART = [0, 0, 0, 1, 1, 2]
    K_PART = [0, 1, 2, 0, 1, 0]
    RUNS = [(0, 3), (3, 5), (5, 6)]
    NZ = len(Q_PART)
    M_ROW = NZ * DH
    ROWS = M_ROW + 3
    ZERO_ROWS = [(32, 64), (64, 128)]

    def pieces(chunk):
        if chunk < 4:
            return [(chunk, 0, 0), (chunk, 1, 512), (chunk, 7, 960)]
        if chunk < 8:
            return [(chunk - 4, 2, 0), (chunk - 4, 6, 384), (chunk - 4, 3, 512), (chunk - 4, 5, 832)]
        return [(p, 4, 256 * p) for p in range(PH)]

    PLACE = {(p, j): (c, col) for c in range(9) for p, j, col in pieces(c)}

    PV_PARTS = [([0, 7], 3), ([1], 3), ([2, 6], 7), ([3, 5, 4], 8)]
    PV_SLOT = {5: (0, 0, 0), 6: (0, 0, 1), 9: (0, 0, 2), 10: (0, 0, 3),
               14: (0, 1, 0), 15: (0, 1, 1), 0: (-1, 1, 2), 1: (-1, 1, 3)}

    FFN_SLOTS = [8, 9, 12, 14]
    LOADS = 16 * 2 * len(RUNS)

    CONSTS = 8 * 16
    N_PV = 8
    N_MAX = 2 * SLOTS

    def row(b, off):
        return 2 * b[0] + (b[1] + off) if isinstance(b, tuple) else b + off

    def at(n_per_row, b, off, j):
        if isinstance(b, tuple):
            return b[0] * (2 * n_per_row) + ((b[1] + off) * n_per_row + j + 1)
        return min((b + off) * n_per_row + j + 1, B * n_per_row)

    def later(value):
        return not isinstance(value, int) or value > 0

    def value(eng, v):
        return v if isinstance(v, int) else eng.to_reg(v)

    def parts_view(dram, half):
        return dram[half, 0:3 * DH, :].rearrange("(c d) (s n) -> d s c n", c=3, n=S)\
            .rearrange("d s c n -> (d s) c n")

    x_v = x.rearrange("b (t p) d -> b p t d", p=128)
    out_v = out.rearrange("b (t p) d -> b p t d", p=128)

    ctx = ExitStack()
    with ctx:
        def sb(name, shape, dt):
            return ctx.enter_context(nc.sbuf_tensor(name, shape, dt))

        def sem(name):
            return ctx.enter_context(nc.semaphore(name))

        q_stack = [sb(f"q_stack{i}", [128, H * S], bf16) for i in range(2)]
        k_stack = [sb(f"k_stack{i}", [128, H * S], bf16) for i in range(2)]
        probs = sb("probs", [128, 9, 1024], fp32)
        v_pad = [sb(f"v_pad{i}", [128, NBLK, 2 * PH, 32], fp32) for i in range(2)]
        x_in = sb("x_in", [128, TT, D], fp32)
        x_res = sb("x_res", [128, TT, D], fp32)
        out_sb = sb("out_sb", [128, TT, D], fp32)
        xn = sb("xn", [128, TT, D], fp32)
        xnT = [sb(f"xnT{i}", [128, S], fp32) for i in range(2)]
        x_sum = sb("x_sum", [128, 1], fp32)
        x_mean = sb("x_mean", [128, 1], fp32)
        stats = sb("stats", [128, TT, 6], fp32)
        mean_var = sb("mean_var", [128, TT, 2], fp32)
        var_eps = sb("var_eps", [128, TT], fp32)
        rstd = sb("rstd", [128, TT], fp32)
        minus_half = sb("minus_half", [128, TT], fp32)
        rope_a = sb("rope_a", [128, 2, S], fp32)
        rope_b = sb("rope_b", [128, 2, S], fp32)
        parts = sb("parts", [128, 2, 3, S], bf16)
        block_max = sb("block_max", [128, 2, 9, 16], fp32)
        row_max = sb("row_max", [128, 2, PH, NBLK], fp32)
        m_rest = sb("m_rest", [64, KB], fp32)
        m_parts = sb("m_parts", [64, 2, 3, KB], bf16)
        pv_sb = sb("pv_sb", [128, 2, S], fp32)
        numer = sb("numer", [128, S], fp32)
        denom = sb("denom", [128, S], fp32)
        attn = sb("attn", [128, S], fp32)
        zT = sb("zT", [128, S], fp32)
        hT = sb("hT", [128, FC, S], fp32)
        ffnT = [sb(f"ffnT{i}", [128, S], fp32) for i in range(2)]
        w1_sb = [sb(f"w1_sb{i}", [128, F], fp32) for i in range(2)]
        w2_sb = [sb(f"w2_sb{i}", [128, FC, D], fp32) for i in range(2)]
        b1_sb = [sb(f"b1_sb{i}", [128, FC], fp32) for i in range(2)]
        b2_sb = [sb(f"b2_sb{i}", [128, 1], fp32) for i in range(2)]
        wqkv_sb = sb("wqkv_sb", [128, 3 * D], fp32)
        w_rope = sb("w_rope", [128, 4, D], fp32)
        w_out_sb = sb("w_out_sb", [128, D], fp32)
        wr_sb = sb("wr_sb", [128, E], fp32)
        br_sb = sb("br_sb", [1, E], fp32)
        route = sb("route", [1, E], fp32)
        route_max = sb("route_max", [1, 8], fp32)
        route_idx = sb("route_idx", [1, 8], u32)
        ident = sb("ident", [128, 128], fp32)
        cosT = sb("cosT", [128, S], fp32)
        sinT = sb("sinT", [128, S], fp32)
        mask = sb("mask", [128, 3, 128], bf16)

        scores_ps = [ctx.enter_context(nc.psum_tensor(f"scores_ps{i}", [128, 2 * BANK], fp32)) for i in range(2)]
        max_ps = [ctx.enter_context(nc.psum_tensor(f"max_ps{i}", [128, BANK], fp32)) for i in range(2)]
        pv_ps = ctx.enter_context(nc.psum_tensor("pv_ps", [128, BANK], fp32))
        misc_ps = ctx.enter_context(nc.psum_tensor("misc_ps", [128, BANK], fp32))

        const_loaded = sem("const_loaded")
        pool_zeroed = sem("pool_zeroed")
        dve_zeroed = sem("dve_zeroed")
        stack_const = sem("stack_const")
        w_ready = sem("w_ready")
        pad_ready = sem("pad_ready")
        half_ready = sem("half_ready")
        x_loaded = sem("x_loaded")
        res_loaded = sem("res_loaded")
        stats_done = sem("stats_done")
        aggr_done = sem("aggr_done")
        var_done = sem("var_done")
        rstd_done = sem("rstd_done")
        xn_done = sem("xn_done")
        xnT_ps_done = sem("xnT_ps_done")
        xnT_done = sem("xnT_done")
        mean_done = sem("mean_done")
        route_ps_done = sem("route_ps_done")
        route_done = sem("route_done")
        top_done = sem("top_done")
        expert_done = sem("expert_done")
        expert_loaded = sem("expert_loaded")
        proj_done = sem("proj_done")
        rope_done = sem("rope_done")
        rotated = sem("rotated")
        part0_done = sem("part0_done")
        rest_done = sem("rest_done")
        part1_done = sem("part1_done")
        part2_done = sem("part2_done")
        parts_written = [sem(f"parts_written{h}") for h in range(2)]
        zeros_written = sem("zeros_written")
        stack_loaded = [sem(f"stack_loaded{h}") for h in range(2)]
        max_mm_done = sem("max_mm_done")
        block_max_done = sem("block_max_done")
        row_max_done = sem("row_max_done")
        maxT_done = sem("maxT_done")
        m_split = sem("m_split")
        m_rows_loaded = [sem(f"m_rows_loaded{h}") for h in range(2)]
        scores_done = sem("scores_done")
        exp_done = sem("exp_done")
        v_ps_done = sem("v_ps_done")
        v_done = sem("v_done")
        pv_done = sem("pv_done")
        pv_copied = sem("pv_copied")
        pv_written = sem("pv_written")
        gathered = sem("gathered")
        recip_done = sem("recip_done")
        attn_done = sem("attn_done")
        proj_out_done = sem("proj_out_done")
        z_done = sem("z_done")
        zT_done = sem("zT_done")
        out_done = sem("out_done")
        ffn1_done = sem("ffn1_done")
        relu_done = sem("relu_done")
        ffn2_done = sem("ffn2_done")
        ffn_done = sem("ffn_done")
        stored = sem("stored")

        block = ctx.enter_context(nc.Block())

        def rows(eng, step):
            for b in range(-3, 1):
                step(b, b % 2, lambda off, b=b: 0 <= b + off < B)
            with eng.Fori(0, (B - 4) // 2) as i:
                step((i, 1), 1, lambda off: True)
                step((i, 2), 0, lambda off: True)
            for b in range(B - 3, B + 1):
                step(b, b % 2, lambda off, b=b: 0 <= b + off < B)

        @block.sync
        def _(sp):
            sp.dma_start(wqkv_sb[:, :], w_qkv).then_inc(const_loaded, 16)
            sp.dma_start(ident[:, :], ident_dram).then_inc(const_loaded, 16)
            sp.dma_start(wr_sb[:, :], Wr).then_inc(const_loaded, 16)
            sp.dma_start(br_sb[:, :], br.rearrange("(a e) -> a e", a=1)).then_inc(const_loaded, 16)
            sp.dma_start(cosT[:, :], cos_dram).then_inc(const_loaded, 16)
            sp.dma_start(sinT[:, :], sin_dram).then_inc(const_loaded, 16)
            sp.dma_start(w_out_sb[:, :], w_out).then_inc(const_loaded, 16)
            sp.dma_start(mask[:, :, :], mask_dram).then_inc(const_loaded, 16)
            for half in range(2):
                sp.dma_start(q_parts_dram[half, 3 * DH:3 * DH + 3, :], zeros_dram).then_inc(zeros_written, 16)
            sp.wait_ge(pool_zeroed, 6)
            sp.wait_ge(dve_zeroed, 2)
            for i in range(2):
                sp.dma_start(k_stack[i][M_ROW:ROWS, :], ones_dram).then_inc(stack_const, 16)

            sp.wait_ge(zeros_written, 32)

            def write_parts(b, half):
                loaded, split = value(sp, at(LOADS, b, 1, LOADS - 1)), value(sp, at(2, b, 2, 1))
                if later(loaded):
                    sp.wait_ge(stack_loaded[half], loaded)
                sp.wait_ge(part2_done, split)
                for qk, dram in enumerate((q_parts_dram, k_parts_dram)):
                    sp.dma_start(parts_view(dram, half), parts[64 * half:64 * half + 64, qk, :, :])\
                      .then_inc(parts_written[half], 16)

            def load_stack(b, off, half, par, last_use):
                free, written = value(sp, last_use), value(sp, at(32, b, off, 31))
                if later(free):
                    sp.wait_ge(scores_done, free)
                sp.wait_ge(parts_written[half], written)
                cols = slice(half * HALF_COLS, (half + 1) * HALF_COLS)
                for z0, z1 in RUNS:
                    n = z1 - z0
                    sp.dma_start(k_stack[par][DH * z0:DH * z1, cols], k_parts_dram[half, 0:DH * n, :])\
                      .then_inc(stack_loaded[half], 16)
                    q0 = DH * Q_PART[z0]
                    if n > 1:
                        sp.dma_start(q_stack[par][DH * z0:DH * z1, cols],
                                     q_parts_dram[half, q0:q0 + DH, :].unsqueeze(0)
                                     .to_broadcast([n, DH, HALF_COLS])).then_inc(stack_loaded[half], 16)
                    else:
                        sp.dma_start(q_stack[par][DH * z0:ROWS, cols], q_parts_dram[half, q0:q0 + DH + 3, :])\
                          .then_inc(stack_loaded[half], 16)

            def load_m_rows(b, off, half, par):
                sp.wait_ge(m_split, at(8, b, off, 4 * half + 3))
                for part in range(3):
                    sp.dma_start(q_stack[par][M_ROW + part:M_ROW + part + 1, half * HALF_COLS:(half + 1) * HALF_COLS]
                                 .rearrange("c (g q) -> c g q", q=KB), m_parts[:, half, part, :])\
                      .then_inc(m_rows_loaded[half], 16)

            def write_pv(half):
                sp.dma_start(pv_dram[128 * half:128 * half + 128, :], pv_sb[:, half, :]).then_inc(pv_written, 16)

            def gather(b, off):
                sp.wait_ge(pv_written, at(32, b, off, 31))
                src = pv_dram.rearrange("(a e r) n -> e a r n", e=2, r=16)
                for e, dst in enumerate((numer, denom)):
                    sp.dma_start(dst[:, :], src[e]).then_inc(gathered, 16)

            def step(b, par, has):
                if has(1):
                    load_stack(b, 1, 1, 1 - par, at(SLOTS, b, -1, 17))
                if has(3):
                    if later(v := at(TT, b, 2, TT - 1)):
                        sp.wait_ge(xn_done, v)
                    sp.dma_start(x_in[:, :, :], x_v[row(b, 3), :, :, :]).then_inc(x_loaded, 16)
                if has(0):
                    load_m_rows(b, 0, 1, par)
                if has(-1):
                    sp.wait_ge(pv_copied, at(2, b, -1, 1))
                    write_pv(1)
                    gather(b, -1)
                if has(2):
                    first, second = value(sp, at(1, b, 0, 0)), value(sp, at(1, b, 2, 0))
                    sp.wait_ge(const_loaded, CONSTS)
                    if later(first):
                        sp.wait_ge(ffn2_done, first)
                    sp.wait_ge(expert_done, second)
                    e = sp.value_load(route_idx[0:1, 0:1], min_val=0, max_val=E - 1)
                    sp.dma_start(w1_sb[par][:, :], W1[e, :, :]).then_inc(expert_loaded, 16)
                    sp.dma_start(w2_sb[par][:, :, :], W2[e, :, :].rearrange("(c p) d -> p c d", p=128))\
                      .then_inc(expert_loaded, 16)
                    with nc.allow_non_contiguous_dma(reason="a bias value per partition"):
                        sp.dma_start(b1_sb[par][:, :], b1[e, :].rearrange("(c p) -> p c", p=128))\
                          .then_inc(expert_loaded, 16)
                        sp.dma_start(b2_sb[par][:, :], b2[e, :].rearrange("(p c) -> p c", c=1))\
                          .then_inc(expert_loaded, 16)
                if has(2):
                    for half in range(2):
                        write_parts(b, half)
                if has(1):
                    load_m_rows(b, 1, 0, 1 - par)
                if has(0):
                    first, second = value(sp, at(1, b, -1, 0)), value(sp, at(2, b, 0, 0))
                    if later(first):
                        sp.wait_ge(attn_done, first)
                    sp.wait_ge(pv_copied, second)
                    write_pv(0)
                if has(2):
                    load_stack(b, 2, 0, par, at(SLOTS, b, 0, 8))
                if has(-1):
                    sp.wait_ge(out_done, at(1, b, -1, 0))
                    sp.dma_start(out_v[row(b, -1), :, :, :], out_sb[:, :, :]).then_inc(stored, 16)
                if has(0):
                    if later(v := at(16, b, -1, 15)):
                        sp.wait_ge(stored, v)
                    sp.dma_start(x_res[:, :, :], x_v[row(b, 0), :, :, :]).then_inc(res_loaded, 16)

            rows(sp, step)
            sp.wait_ge(stored, 16 * B)

        @block.gpsimd
        def _(pool):
            for n, stack in enumerate((q_stack[0], k_stack[0], q_stack[1])):
                for i, (r0, r1) in enumerate(ZERO_ROWS):
                    if later(v := 2 * n + i):
                        pool.wait_ge(pool_zeroed, v)
                    pool.memset(stack[r0:r1, :].bitcast(fp32), 0.0).then_inc(pool_zeroed, 1)
            pool.wait_ge(pool_zeroed, 6)
            pool.memset(minus_half[:, :], -0.5).then_inc(half_ready, 1)
            pool.wait_ge(half_ready, 1)
            pads = [(0, 8, 0.0), (64, 0, 0.0), (0, 16, 1.0), (64, 16, 0.0), (0, 24, 0.0), (64, 24, 1.0)]
            for n in range(12):
                first, col, fill = pads[n % 6]
                if later(v := n):
                    pool.wait_ge(pad_ready, v)
                pool.memset(v_pad[n // 6][first:first + 64, :, :, col:col + 8], fill).then_inc(pad_ready, 1)
            pool.wait_ge(pad_ready, 12)

            def step(b, par, has):
                if has(2):
                    def rotate(qk):
                        pool.wait_ge(rope_done, at(4, b, 2, 2 * qk + 1))
                        pool.tensor_tensor(rope_a[:, qk, :], rope_a[:, qk, :], rope_b[:, qk, :], ALU.add)\
                            .then_inc(rotated, 1)

                    def rest(qk):
                        pool.wait_ge(part0_done, at(2, b, 2, qk))
                        pool.tensor_tensor(rope_b[:, qk, :], rope_a[:, qk, :], parts[:, qk, 0, :], ALU.subtract)\
                            .then_inc(rest_done, 1)

                    def last_part(qk):
                        pool.wait_ge(part1_done, at(2, b, 2, qk))
                        pool.tensor_tensor(parts[:, qk, 2, :], rope_b[:, qk, :], parts[:, qk, 1, :], ALU.subtract)\
                            .then_inc(part2_done, 1)

                    rotate(0)
                    rest(0)
                    rotate(1)
                    last_part(0)
                    rest(1)
                    last_part(1)
                if has(3):
                    pool.wait_ge(var_done, at(1, b, 3, 0))
                    pool.tensor_tensor(rstd[:, :], var_eps[:, :], minus_half[:, :], ALU.pow).then_inc(rstd_done, 1)

            rows(pool, step)

        @block.scalar
        def _(act):
            act.wait_ge(pad_ready, 12)

            def exp(b, k):
                act.wait_ge(scores_done, at(SLOTS, b, 0, k))
                last = 1 if k % 9 < 4 else 3
                if later(v := at(N_PV, b, 0, last) if k >= 9 else at(N_PV, b, -1, 4 + last)):
                    act.wait_ge(pv_done, v)
                nc.scalar.activation(probs[:, k % 9, :], scores_ps[k % 2][:, :], ACT.Exp, scale=SCALE)\
                  .then_inc(exp_done, 1)

            def copy_pv(b, off, half):
                act.wait_ge(pv_done, at(N_PV, b, off, 4 * half + 3))
                nc.scalar.activation(pv_sb[:, half, :], pv_ps[:, :], ACT.Copy).then_inc(pv_copied, 1)

            def relu(b, par, c):
                act.wait_ge(ffn1_done, at(FC, b, 1, c))
                nc.scalar.activation(hT[:, c, :], misc_ps[:, :], ACT.Relu, bias=b1_sb[1 - par][:, c:c + 1])\
                  .then_inc(relu_done, 1)

            def part(b, qk, i):
                src = rope_a if i == 0 else rope_b
                act.wait_ge(rotated if i == 0 else rest_done, at(2, b, 2, qk))
                if i == 0 and qk == 0:
                    for half in range(2):
                        if later(v := at(32, b, 1, 31)):
                            act.wait_ge(parts_written[half], v)
                nc.scalar.activation(parts[:, qk, i, :], src[:, qk, :], ACT.Copy)\
                  .then_inc(part0_done if i == 0 else part1_done, 1)

            def step(b, par, has):
                for k in range(SLOTS):
                    if has(0):
                        exp(b, k)
                    if k == 0 and has(2):
                        if later(v := at(1, b, 1, 0)):
                            act.wait_ge(mean_done, v)
                        act.wait_ge(xnT_ps_done, at(1, b, 2, 0))
                        nc.scalar.activation(xnT[par][:, :], misc_ps[:, :], ACT.Identity, accum_out=x_sum[:, :])\
                          .then_inc(xnT_done, 1)
                    if k == 2 and has(-1):
                        copy_pv(b, -1, 1)
                    if k == 3 and has(1):
                        act.wait_ge(v_ps_done, at(1, b, 1, 0))
                        for r in range(2):
                            nc.scalar.activation(
                                v_pad[1 - par][64 * r:64 * r + 64, :, :, 8 * r:8 * r + 8],
                                misc_ps[64 * r:64 * r + 64, :].rearrange("k (j p d) -> k j p d", j=NBLK, d=DH),
                                ACT.Copy).then_inc(v_done, 1)
                    if k == 7 and has(2):
                        part(b, 0, 0)
                    if k == 9 and has(2):
                        part(b, 0, 1)
                        part(b, 1, 0)
                    if k in FFN_SLOTS and has(1):
                        relu(b, par, FFN_SLOTS.index(k))
                    if k == 11 and has(0):
                        copy_pv(b, 0, 0)
                    if k == 11 and has(2):
                        part(b, 1, 1)
                    if k == 16 and has(1):
                        if later(v := at(1, b, -1, 0)):
                            act.wait_ge(z_done, v)
                        act.wait_ge(ffn2_done, at(1, b, 1, 0))
                        nc.scalar.activation(ffnT[1 - par][:, :], misc_ps[:, :], ACT.Identity,
                                             bias=b2_sb[1 - par][:, 0:1]).then_inc(ffn_done, 1)

            rows(act, step)

        @block.tensor
        def _(pe):
            pe.wait_ge(const_loaded, CONSTS)
            pe.wait_ge(w_ready, 12)

            def slot_cols(half, r, p):
                return (half * 8 + r * PH + p) * S

            def bank_blocks(ps, bank, chunk, half, stat, mov, transposed):
                here = [(p, j, col - BANK * bank) for p, j, col in pieces(chunk) if col // BANK == bank]
                diag = [(col if transposed else col + S - KB * j - KB) // KB for _, j, col in here]
                n = len(diag)
                step = diag[-1] - diag[0] if n == 2 else 1
                diagonals = ps.rearrange("p (a n) -> p a n", n=KB)[:, diag[0]:diag[-1] + 1:step, :]
                nc.tensor.matmul(diagonals, mask[:, 0 if transposed else 1, :],
                                 mask[:, 2, 0:n * KB].rearrange("k (a n) -> k a n", n=KB),
                                 start=True, stop=False, skip_group_check=True)
                for n, (p, j, col) in enumerate(here):
                    width = S - KB * j
                    stat_at = KB * (j if transposed else NBLK - 1 - j)
                    mov_at = KB * j if transposed else 0
                    for r in range(2):
                        c = slot_cols(half, r, p)
                        last = nc.tensor.matmul(ps[64 * r:64 * r + 64, col:col + width],
                                                stat[:, c + stat_at:c + stat_at + KB],
                                                mov[:, c + mov_at:c + mov_at + width],
                                                start=False, stop=(n == len(here) - 1), skip_group_check=True)
                return last

            def scores(b, par, k):
                if k % 9 == 0:
                    pe.wait_ge(m_rows_loaded[k // 9], at(48, b, 0, 47))
                if later(v := at(SLOTS, b, 0, k - 2)):
                    pe.wait_ge(exp_done, v)
                for bank in range(2):
                    last = bank_blocks(scores_ps[k % 2][:, bank * BANK:(bank + 1) * BANK], bank, k % 9, k // 9,
                                       k_stack[par], q_stack[par], True)
                last.then_inc(scores_done, 1)

            def max_scores(b, par, k):
                if k % 9 == 0:
                    pe.wait_ge(stack_loaded[k // 9], at(LOADS, b, 1, LOADS - 1))
                    pe.wait_ge(stack_const, 32)
                for bank in range(2):
                    if later(v := at(N_MAX, b, 1, 2 * k + bank - 2)):
                        pe.wait_ge(block_max_done, v)
                    bank_blocks(max_ps[bank][:, :], bank, k % 9, k // 9, q_stack[1 - par],
                                k_stack[1 - par], False).then_inc(max_mm_done, 1)

            def pv(b, off, par, half, i):
                blocks, chunk = PV_PARTS[i]
                if i == 0:
                    pe.wait_ge(v_done, at(2, b, off, 1))
                    if later(v := at(2, b, off, half - 1)):
                        pe.wait_ge(pv_copied, v)
                pe.wait_ge(exp_done, at(SLOTS, b, off, 9 * half + chunk))
                for j in blocks:
                    for p in range(PH):
                        ch, col = PLACE[p, j]
                        last = nc.tensor.matmul(pv_ps[32 * p:32 * p + 32, KB * j:S],
                                                v_pad[par][:, j, PH * half + p, :],
                                                probs[:, ch, col:col + S - KB * j],
                                                start=(j == 0), stop=(j == 4), skip_group_check=True)
                last.then_inc(pv_done, 1)

            def transpose_max(b, off, half):
                pe.wait_ge(row_max_done, at(16, b, off, 8 * half + 7))
                for r in range(2):
                    last = nc.tensor.matmul(misc_ps[32 * r:32 * r + 32, 0:KB],
                                            row_max[:, half, :, :].rearrange("q p i -> q (p i)"),
                                            ident[:, KB * r:KB * r + KB], start=True, stop=True)
                last.then_inc(maxT_done, 1)

            def misc(b, par, k, has):
                if k == 0 and has(2):
                    if later(v := at(1, b, 0, 0)):
                        pe.wait_ge(ffn_done, v)
                    pe.wait_ge(xn_done, at(TT, b, 2, TT - 1))
                    for t in range(TT):
                        last = nc.tensor.transpose(misc_ps[:, 128 * t:128 * t + 128], xn[:, t, :], ident[:, :])
                    last.then_inc(xnT_ps_done, 1)
                if k == 1 and has(0):
                    pe.wait_ge(xnT_done if has(2) else ffn_done, at(1, b, 2 if has(2) else 0, 0))
                    transpose_max(b, 0, 1)
                if k == 2 and has(2):
                    if later(v := at(8, b, 0, 5)):
                        pe.wait_ge(m_split, v)
                    pe.wait_ge(mean_done, at(1, b, 2, 0))
                    nc.tensor.matmul(misc_ps[0:1, 0:E], x_mean[:, :], wr_sb[:, :], start=True, stop=True)\
                      .then_inc(route_ps_done, 1)
                if k == 3 and has(1):
                    pe.wait_ge(route_done, at(1, b, 2, 0))
                    if later(v := at(8, b, 0, 5)):
                        pe.wait_ge(m_split, v)
                    for j in range(NBLK):
                        for r in range(2):
                            last = nc.tensor.matmul(
                                misc_ps[64 * r:64 * r + 64, KB * j:KB * j + KB],
                                xnT[1 - par][:, KB * j:KB * j + KB],
                                wqkv_sb[:, 2 * D:3 * D].rearrange("k (p r d) -> k p r d", r=2, d=DH)[:, :, r, :],
                                start=True, stop=True)
                    last.then_inc(v_ps_done, 1)
                if 4 <= k < 8 and has(2):
                    if k == 4:
                        if later(v := at(2, b, 1, 1)):
                            pe.wait_ge(v_done, v)
                        pe.wait_ge(route_done, at(1, b, 2, 0))
                    elif later(v := at(4, b, 2, k - 5)):
                        pe.wait_ge(rope_done, v)
                    nc.tensor.matmul(misc_ps[:, :], w_rope[:, k - 4, :], xnT[par][:, :], start=True, stop=True)\
                      .then_inc(proj_done, 1)
                if k in FFN_SLOTS and has(1):
                    c = FFN_SLOTS.index(k)
                    if c == 0:
                        pe.wait_ge(v_done, at(2, b, 1, 1))
                        pe.wait_ge(rope_done, at(4, b, 2, 3))
                        pe.wait_ge(expert_loaded, at(64, b, 1, 63))
                    if c == 1:
                        pe.wait_ge(relu_done, at(FC, b, 1, 0))
                    if c == 2:
                        if later(v := at(1, b, -1, 0)):
                            pe.wait_ge(z_done, v)
                        else:
                            pe.wait_ge(m_split, at(8, b, 1, 1))
                    if c == 3:
                        pe.wait_ge(relu_done, at(FC, b, 1, 2))
                        if later(v := at(1, b, -1, 0)):
                            pe.wait_ge(out_done, v)
                    nc.tensor.matmul(misc_ps[:, :], w1_sb[1 - par][:, 128 * c:128 * c + 128], xnT[1 - par][:, :],
                                     start=True, stop=True).then_inc(ffn1_done, 1)
                if k == 10 and has(1):
                    pe.wait_ge(relu_done, at(FC, b, 1, 1))
                    transpose_max(b, 1, 0)
                if k == 11 and has(-1):
                    if has(1):
                        pe.wait_ge(m_split, at(8, b, 1, 1))
                    elif has(0):
                        pe.wait_ge(m_split, at(8, b, 0, 5))
                    else:
                        pe.wait_ge(out_done, at(1, b, -2, 0))
                    pe.wait_ge(attn_done, at(1, b, -1, 0))
                    nc.tensor.matmul(misc_ps[:, :], w_out_sb[:, :], attn[:, :], start=True, stop=True)\
                      .then_inc(proj_out_done, 1)
                if k == 13 and has(-1):
                    if has(1):
                        pe.wait_ge(relu_done, at(FC, b, 1, 2))
                    pe.wait_ge(z_done, at(1, b, -1, 0))
                    for t in range(TT):
                        last = nc.tensor.transpose(misc_ps[:, 128 * t:128 * t + 128],
                                                   zT[:, 128 * t:128 * t + 128], ident[:, :])
                    last.then_inc(zT_done, 1)
                if k in (15, 16) and has(1):
                    if k == 15:
                        pe.wait_ge(relu_done, at(FC, b, 1, FC - 1))
                    for c in (0, 1) if k == 15 else (2, 3):
                        last = nc.tensor.matmul(misc_ps[:, :], w2_sb[1 - par][:, c, :], hT[:, c, :],
                                                start=(c == 0), stop=(c == FC - 1))
                    if k == 16:
                        last.then_inc(ffn2_done, 1)

            def step(b, par, has):
                for k in range(SLOTS):
                    if has(0):
                        scores(b, par, k)
                    if k in PV_SLOT and has(PV_SLOT[k][0]):
                        off, half, i = PV_SLOT[k]
                        pv(b, off, par if off == 0 else 1 - par, half, i)
                    if has(1):
                        max_scores(b, par, k)
                    misc(b, par, k, has)

            rows(pe, step)

        @block.vector
        def _(dve):
            for r0, r1 in ZERO_ROWS:
                nc.vector.memset(k_stack[1][r0:r1, :].bitcast(fp32), 0.0).then_inc(dve_zeroed, 1)
            dve.wait_ge(const_loaded, CONSTS)
            for qk in range(2):
                for half in range(2):
                    src = wqkv_sb[:, qk * D + 64 * half:qk * D + 64 * half + 64]\
                        .rearrange("k (p r d) -> k d r p", r=2, d=DH)
                    plain, swapped = (w_rope[:, 2 * qk + i, 64 * half:64 * half + 64]
                                      .rearrange("k (d r p) -> k d r p", r=2, d=DH) for i in range(2))
                    nc.vector.tensor_copy(plain, src).then_inc(w_ready, 1)
                    nc.vector.tensor_copy(swapped[:, 0:4, :, :], src[:, 4:8, :, :]).then_inc(w_ready, 1)
                    nc.vector.tensor_copy(swapped[:, 4:8, :, :], src[:, 0:4, :, :]).then_inc(w_ready, 1)

            def block_maxima(b, k):
                for bank in range(2):
                    dve.wait_ge(max_mm_done, at(N_MAX, b, 1, 2 * k + bank))
                    nc.vector.tensor_reduce(block_max[:, k // 9, k % 9, 8 * bank:8 * bank + 8],
                                            max_ps[bank][:, :].rearrange("q (a c) -> q a c", c=KB),
                                            AX.X, ALU.max).then_inc(block_max_done, 1)

            def row_maxima(b, off, half):
                dve.wait_ge(block_max_done, at(N_MAX, b, off, 18 * half + 17))
                for j in range(NBLK):
                    chunk, col = PLACE[0, j]
                    n, a = NBLK - j, col // KB
                    if chunk == 8:
                        src = block_max[:, half, 8, :].rearrange("q (p a) -> q p a", p=PH)
                    else:
                        src = block_max[:, half, chunk:chunk + PH, a:a + n]
                    nc.vector.tensor_reduce(row_max[:, half, :, NBLK - 1 - j], src, AX.X, ALU.max)\
                      .then_inc(row_max_done, 1)

            def split_max(b, off, half):
                mT = misc_ps[0:64, 0:KB]
                if later(v := at(48, b, off - 1, 47)):
                    dve.wait_ge(m_rows_loaded[half], v)
                dve.wait_ge(maxT_done, at(2, b, off, half))
                nc.vector.tensor_scalar(m_parts[:, half, 0, :], mT, -1.0, None, ALU.mult).then_inc(m_split, 1)
                dve.wait_ge(m_split, at(8, b, off, 4 * half))
                nc.vector.scalar_tensor_tensor(out=m_rest[:, :], in0=mT, scalar=-1.0, in1=m_parts[:, half, 0, :],
                                               op0=ALU.mult, op1=ALU.subtract).then_inc(m_split, 1)
                dve.wait_ge(m_split, at(8, b, off, 4 * half + 1))
                nc.vector.tensor_copy(m_parts[:, half, 1, :], m_rest[:, :]).then_inc(m_split, 1)
                dve.wait_ge(m_split, at(8, b, off, 4 * half + 2))
                nc.vector.tensor_tensor(m_parts[:, half, 2, :], m_rest[:, :], m_parts[:, half, 1, :],
                                        ALU.subtract).then_inc(m_split, 1)

            def rope(b, i):
                dve.wait_ge(proj_done, at(4, b, 2, i))
                dst, table = ((rope_a, cosT), (rope_b, sinT))[i % 2]
                if i % 2:
                    if later(v := at(2, b, 1, i // 2)):
                        dve.wait_ge(part2_done, v)
                nc.vector.tensor_tensor(dst[:, i // 2, :], misc_ps[:, :], table[:, :], ALU.mult)\
                  .then_inc(rope_done, 1)

            def router(b):
                dve.wait_ge(route_ps_done, at(1, b, 2, 0))
                nc.vector.tensor_tensor(route[:, :], misc_ps[0:1, 0:E], br_sb[:, :], ALU.add)\
                  .then_inc(route_done, 1)
                done = value(dve, at(1, b, 2, 0))
                dve.wait_ge(const_loaded, CONSTS)
                dve.wait_ge(route_done, done)
                nc.vector.max(route_max[:, :], route[:, :]).then_inc(top_done, 1)
                loaded = value(dve, at(64, b, 1, 63))
                dve.wait_ge(const_loaded, CONSTS)
                dve.wait_ge(top_done, done)
                if later(v := loaded):
                    dve.wait_ge(expert_loaded, v)
                nc.vector.max_index(route_idx[:, :], route_max[:, :], route[:, :]).then_inc(expert_done, 1)

            def reciprocals(b, quarter):
                cols = slice(128 * quarter, 128 * quarter + 128)
                if quarter == 0:
                    dve.wait_ge(gathered, at(32, b, -1, 31))
                nc.vector.reciprocal(denom[:, cols], denom[:, cols]).then_inc(recip_done, 1)

            def normalise(b):
                dve.wait_ge(recip_done, at(4, b, -1, 3))
                nc.vector.tensor_tensor(attn[:, :], numer[:, :], denom[:, :], ALU.mult).then_inc(attn_done, 1)

            def ln_stats(b):
                dve.wait_ge(x_loaded, at(16, b, 3, 15))
                for t in range(TT):
                    nc.vector.bn_stats(stats[:, t, :], x_in[:, t, :]).then_inc(stats_done, 1)
                for t in range(TT):
                    done = value(dve, at(TT, b, 3, t))
                    dve.wait_ge(const_loaded, CONSTS)
                    dve.wait_ge(stats_done, done)
                    nc.vector.bn_aggr(mean_var[:, t, :], stats[:, t, :]).then_inc(aggr_done, 1)
                dve.wait_ge(aggr_done, at(TT, b, 3, TT - 1))
                nc.vector.tensor_scalar(var_eps[:, :], mean_var[:, :, 1], EPS, None, ALU.add).then_inc(var_done, 1)

            def ln_apply(b):
                dve.wait_ge(rstd_done, at(1, b, 3, 0))
                if later(v := at(1, b, 2, 0)):
                    dve.wait_ge(xnT_ps_done, v)
                for t in range(TT):
                    nc.vector.tensor_scalar(xn[:, t, :], x_in[:, t, :], mean_var[:, t, 0:1], rstd[:, t:t + 1],
                                            ALU.subtract, ALU.mult).then_inc(xn_done, 1)

            def step(b, par, has):
                for k in range(SLOTS):
                    if k == 0 and has(0):
                        row_maxima(b, 0, 1)
                    if has(1):
                        block_maxima(b, k)
                    if k == 0 and has(2):
                        dve.wait_ge(xnT_done, at(1, b, 2, 0))
                        nc.vector.tensor_scalar(x_mean[:, :], x_sum[:, :], 1.0 / S, None, ALU.mult)\
                          .then_inc(mean_done, 1)
                    if k == 1 and has(0):
                        split_max(b, 0, 1)
                    if k == 2 and has(2):
                        router(b)
                    if 4 <= k < 8 and has(2):
                        rope(b, k - 4)
                    if 6 <= k < 10 and has(-1):
                        reciprocals(b, k - 6)
                    if k == 9 and has(1):
                        row_maxima(b, 1, 0)
                    if k == 10 and has(1):
                        split_max(b, 1, 0)
                    if k == 10 and has(-1):
                        normalise(b)
                    if k == 11 and has(-1):
                        dve.wait_ge(proj_out_done, at(1, b, -1, 0))
                        dve.wait_ge(ffn_done, at(1, b, -1, 0))
                        nc.vector.tensor_tensor(zT[:, :], misc_ps[:, :], ffnT[1 - par][:, :], ALU.add)\
                          .then_inc(z_done, 1)
                    if k == 12 and has(3):
                        ln_stats(b)
                    if k == 13 and has(-1):
                        dve.wait_ge(zT_done, at(1, b, -1, 0))
                        dve.wait_ge(res_loaded, at(16, b, -1, 15))
                        nc.vector.tensor_tensor(out_sb[:, :, :], misc_ps[:, :].rearrange("p (t d) -> p t d", d=D),
                                                x_res[:, :, :], ALU.add).then_inc(out_done, 1)
                    if k == 15 and has(3):
                        ln_apply(b)

            rows(dve, step)


_INS = ['L0_attn_x', 'L0_attn_w_qkv', 'L0_attn_w_out', 'L0_ffn_Wr', 'L0_ffn_br', 'L0_ffn_W1', 'L0_ffn_b1',
        'L0_ffn_W2', 'L0_ffn_b2']
_OUTS = [((16, 512, 128), 'float32')]


def _constants():
    import numpy as np
    from concourse import mybir
    bf16 = mybir.dt.np(mybir.dt.bfloat16)
    S, DH, KB, MASKED = 512, 8, 64, -1e30
    ident = np.eye(128, dtype=np.float32)
    inv_freq = (1.0 / np.float32(10000.0) ** (np.arange(0, DH, 2, dtype=np.float32) / DH)).astype(np.float32)
    freqs = np.arange(S, dtype=np.float32)[:, None] * inv_freq[None, :]
    cos, sin = np.cos(freqs).astype(np.float32), np.sin(freqs).astype(np.float32)
    d = (np.arange(128) % 64) // 8
    cosT = np.ascontiguousarray(cos[:, d % 4].T)
    sinT = np.ascontiguousarray(sin[:, d % 4].T * np.where(d < 4, -1, 1)[:, None].astype(np.float32))
    n, m = np.arange(128)[:, None], np.arange(128)[None, :] % KB
    mask = np.stack([np.where(m > n, MASKED, 0.0), np.where(n > m, MASKED, 0.0), n == m], axis=1)
    mask[KB:] = 0.0
    return {"ident": ident, "cos": cosT, "sin": sinT, "mask": mask.astype(bf16),
            "ones": np.ones((3, 16 * S), bf16), "zeros": np.zeros((3, 8 * S), bf16)}


def kernel(**inputs):
    import numpy as _np
    import concourse.bacc as _bacc
    from concourse import mybir as _mybir
    from concourse.bass_utils import run_bass_kernel_spmd as _run

    nc = _bacc.Bacc("TRN2", target_bir_lowering=False, num_devices=1)
    arrays, args = {}, []
    named = {name: inputs[name] for name in _INS} | _constants()
    for name, a in named.items():
        a = _np.ascontiguousarray(a)
        arrays[f"in_{name}_dram"] = a
        args.append(nc.dram_tensor(f"in_{name}_dram", a.shape, _mybir.dt.from_np(a.dtype), kind="ExternalInput").ap())
    for i, (shape, dtype) in enumerate(_OUTS):
        dt = _mybir.dt.from_np(_np.dtype(dtype))
        args.append(nc.dram_tensor(f"out_{i}_dram", shape, dt, kind="ExternalOutput").ap())
    out = args.pop()
    for name, rows in (("q_parts_dram", 27), ("k_parts_dram", 24)):
        args.append(nc.dram_tensor(name, (2, rows, 4096), _mybir.dt.bfloat16, kind="Internal").ap())
    args.append(nc.dram_tensor("pv_dram", (256, 512), _mybir.dt.float32, kind="Internal").ap())
    layernorm_attention_moe_kernel(nc, *args, out)
    r = _run(nc, [arrays], core_ids=[0])
    got = tuple(r.results[0][f"out_{i}_dram"] for i in range(len(_OUTS)))
    return got[0]
```

```python
import concourse.bass as bass
from concourse import mybir
from contextlib import ExitStack


def layernorm_attention_moe_kernel(
    nc: bass.Bass,
    x: bass.AP,
    w_qkv: bass.AP,
    w_out: bass.AP,
    Wr: bass.AP,
    br: bass.AP,
    W1: bass.AP,
    b1: bass.AP,
    W2: bass.AP,
    b2: bass.AP,
    ident_dram: bass.AP,
    cos_dram: bass.AP,
    sin_dram: bass.AP,
    mask_dram: bass.AP,
    ones_dram: bass.AP,
    zeros_dram: bass.AP,
    q_parts_dram: bass.AP,
    k_parts_dram: bass.AP,
    pv_dram: bass.AP,
    out: bass.AP,
):
    fp32 = mybir.dt.float32
    fp32r = mybir.dt.float32r
    bf16 = mybir.dt.bfloat16
    u32 = mybir.dt.uint32
    ALU = mybir.AluOpType
    ACT = mybir.ActivationFunctionType
    AX = mybir.AxisListType

    B, S, D = x.shape
    E, _, F = W1.shape
    H = 16
    DH = D // H
    SCALE = float(DH) ** -0.5
    EPS = 1e-5
    TT = S // 128
    FC = F // 128
    KB = 64
    NBLK = S // KB
    PH = 4
    SLOTS = 18
    BANK = 512
    HALF_COLS = 2 * PH * S

    Q_PART = [0, 0, 0, 1, 1, 2]
    K_PART = [0, 1, 2, 0, 1, 0]
    RUNS = [(0, 3), (3, 5), (5, 6)]
    NZ = len(Q_PART)
    M_ROW = NZ * DH
    ROWS = M_ROW + 3
    ZERO_ROWS = [(32, 64), (64, 128)]

    def pieces(chunk):
        if chunk < 4:
            return [(chunk, 0, 0), (chunk, 1, 512), (chunk, 7, 960)]
        if chunk < 8:
            return [(chunk - 4, 2, 0), (chunk - 4, 6, 384), (chunk - 4, 3, 512), (chunk - 4, 5, 832)]
        return [(p, 4, 256 * p) for p in range(PH)]

    PLACE = {(p, j): (c, col) for c in range(9) for p, j, col in pieces(c)}

    GROUP_SLOT = {1: (0, 0), 3: (0, 1), 5: (0, 2), 7: (0, 3), 8: (0, 4),
                  10: (1, 0), 12: (1, 1), 14: (1, 2), 16: (1, 3), 17: (1, 4)}
    GROUP_OPS = [2, 2, 3, 3, 1]
    N_MASK = 2 * 2 * sum(GROUP_OPS)

    def masked_after(half, group):
        return half * N_MASK // 2 + 2 * sum(GROUP_OPS[:group + 1])

    PV_PARTS = [([0, 7], 1), ([1], 1), ([2, 6], 3), ([3], 3), ([5, 4], 4)]
    PV_SLOT = {7: (0, 0, 0), 8: (0, 0, 1), 9: (0, 0, 2), 10: (0, 0, 3), 11: (0, 0, 4),
               14: (0, 1, 0), 15: (0, 1, 1), 0: (-1, 1, 2), 2: (-1, 1, 3), 3: (-1, 1, 4)}

    RECIP_SLOTS = [7, 7, 8, 9]
    FFN_SLOTS = [8, 9, 11, 13]

    CONSTS = 7 * 16
    LOADS = 16 * 2 * len(RUNS)
    N_PV = 2 * len(PV_PARTS)
    N_MAX = 2 * SLOTS

    def row(b, off):
        return 2 * b[0] + (b[1] + off) if isinstance(b, tuple) else b + off

    def at(n_per_row, b, off, j):
        if isinstance(b, tuple):
            return b[0] * (2 * n_per_row) + ((b[1] + off) * n_per_row + j + 1)
        return min((b + off) * n_per_row + j + 1, B * n_per_row)

    def later(value):
        return not isinstance(value, int) or value > 0

    def proj_slot(b, i):
        return (1, 2, 2, 2)[i] if b == -2 else 4 + i

    def value(eng, v):
        return v if isinstance(v, int) else eng.to_reg(v)

    def parts_view(dram, half):
        return dram[half, 0:3 * DH, :].rearrange("(c d) (s n) -> (d s) c n", c=3, n=S)

    x_v = x.rearrange("b (t p) d -> b p t d", p=128)
    out_v = out.rearrange("b (t p) d -> b p t d", p=128)

    ctx = ExitStack()
    with ctx:
        def sb(name, shape, dt):
            return ctx.enter_context(nc.sbuf_tensor(name, shape, dt))

        def sem(name):
            return ctx.enter_context(nc.semaphore(name))

        q_stack = [sb(f"q_stack{i}", [128, H * S], bf16) for i in range(2)]
        k_stack = [sb(f"k_stack{i}", [128, H * S], bf16) for i in range(2)]
        probs = sb("probs", [128, 9, 1024], fp32)
        v_pad = [sb(f"v_pad{i}", [128, NBLK, 2 * PH, 32], fp32) for i in range(2)]
        x_in = sb("x_in", [128, TT, D], fp32)
        x_res = sb("x_res", [128, TT, D], fp32)
        out_sb = sb("out_sb", [128, TT, D], fp32)
        xnT = [sb(f"xnT{i}", [128, S], fp32) for i in range(2)]
        x_sum = sb("x_sum", [128, 1], fp32)
        x_mean = sb("x_mean", [128, 1], fp32)
        stats = sb("stats", [128, TT, 6], fp32)
        mean_var = sb("mean_var", [128, TT, 2], fp32)
        var_eps = sb("var_eps", [128, TT], fp32)
        rstd = sb("rstd", [128, TT], fp32)
        minus_half = sb("minus_half", [128, TT], fp32)
        rope_a = sb("rope_a", [128, 2, S], fp32)
        rope_b = sb("rope_b", [128, 2, S], fp32)
        parts = sb("parts", [128, 2, 3, S], bf16)
        block_max = sb("block_max", [128, 2, 9, 16], fp32)
        row_max = sb("row_max", [128, 2, PH, NBLK], fp32)
        m_rest = sb("m_rest", [64, KB], fp32)
        m_parts = sb("m_parts", [64, 2, 3, KB], bf16)
        pv_sb = sb("pv_sb", [128, 2, S], fp32)
        numer = sb("numer", [128, S], fp32)
        denom = sb("denom", [128, S], fp32)
        hT = sb("hT", [128, FC, S], fp32)
        ffn = [sb(f"ffn{i}", [128, TT, D], fp32) for i in range(2)]
        w1_sb = sb("w1_sb", [128, F], fp32)
        w1_hi = sb("w1_hi", [128, F], fp32r)
        w1_lo = sb("w1_lo", [128, F], fp32r)
        w2_sb = [sb(f"w2_sb{i}", [128, FC, D], fp32) for i in range(2)]
        b1_sb = [sb(f"b1_sb{i}", [128, FC], fp32) for i in range(2)]
        b2_sb = [sb(f"b2_sb{i}", [128, D], fp32) for i in range(2)]
        wqkv_sb = sb("wqkv_sb", [128, 3 * D], fp32)
        w_rope_hi = sb("w_rope_hi", [128, 4, D], fp32r)
        w_rope_lo = sb("w_rope_lo", [128, 4, D], fp32r)
        xnT_hi = [sb(f"xnT_hi{i}", [128, S], fp32r) for i in range(2)]
        xnT_lo = [sb(f"xnT_lo{i}", [128, S], fp32r) for i in range(2)]
        w_out_sb = sb("w_out_sb", [128, D], fp32)
        wr_sb = sb("wr_sb", [128, E], fp32)
        br_sb = sb("br_sb", [1, E], fp32)
        route = sb("route", [1, E], fp32)
        route_max = sb("route_max", [1, 8], fp32)
        route_idx = sb("route_idx", [1, 8], u32)
        ident = sb("ident", [128, 128], fp32)
        cosT = sb("cosT", [128, S], fp32)
        sinT = sb("sinT", [128, S], fp32)
        mask = sb("mask", [128, 2, 128], bf16)

        scores_ps = [ctx.enter_context(nc.psum_tensor(f"scores_ps{i}", [128, 2 * BANK], fp32)) for i in range(2)]
        max_ps = [ctx.enter_context(nc.psum_tensor(f"max_ps{i}", [128, BANK], fp32)) for i in range(2)]
        pv_ps = ctx.enter_context(nc.psum_tensor("pv_ps", [128, BANK], fp32))
        misc_ps = ctx.enter_context(nc.psum_tensor("misc_ps", [128, BANK], fp32))

        table_loaded = sem("table_loaded")
        ident_loaded = sem("ident_loaded")
        const_loaded = sem("const_loaded")
        zeroed = sem("zeroed")
        stack_const = [sem(f"stack_const{i}") for i in range(2)]
        w_ready = sem("w_ready")
        pad_ready = sem("pad_ready")
        half_ready = sem("half_ready")
        x_loaded = sem("x_loaded")
        res_loaded = sem("res_loaded")
        stats_done = sem("stats_done")
        aggr_done = sem("aggr_done")
        var_done = sem("var_done")
        rstd_done = sem("rstd_done")
        xn_done = sem("xn_done")
        xnT_ps_done = sem("xnT_ps_done")
        xnT_done = sem("xnT_done")
        hi_done = sem("hi_done")
        lo_done = sem("lo_done")
        w1_hi_done = sem("w1_hi_done")
        w1_lo_done = sem("w1_lo_done")
        mean_done = sem("mean_done")
        route_ps_done = sem("route_ps_done")
        route_done = sem("route_done")
        top_done = sem("top_done")
        expert_done = sem("expert_done")
        expert_loaded = sem("expert_loaded")
        proj_done = sem("proj_done")
        rope_done = sem("rope_done")
        rotated = sem("rotated")
        part0_done = sem("part0_done")
        rest_done = sem("rest_done")
        part1_done = sem("part1_done")
        part2_done = sem("part2_done")
        parts_written = [sem(f"parts_written{h}") for h in range(2)]
        zeros_written = sem("zeros_written")
        stack_loaded = [sem(f"stack_loaded{h}") for h in range(2)]
        max_mm_done = sem("max_mm_done")
        block_max_done = sem("block_max_done")
        row_max_done = sem("row_max_done")
        maxT_done = sem("maxT_done")
        m_split = sem("m_split")
        m_rows_loaded = [sem(f"m_rows_loaded{h}") for h in range(2)]
        scores_done = sem("scores_done")
        exp_done = sem("exp_done")
        masked = sem("masked")
        v_ps_done = sem("v_ps_done")
        v_done = sem("v_done")
        pv_done = sem("pv_done")
        pv_copied = sem("pv_copied")
        pv_written = sem("pv_written")
        gathered = sem("gathered")
        recip_done = sem("recip_done")
        attn_done = sem("attn_done")
        proj_out_done = sem("proj_out_done")
        residual_done = sem("residual_done")
        out_done = sem("out_done")
        ffn1_done = sem("ffn1_done")
        relu_done = sem("relu_done")
        ffn2_done = sem("ffn2_done")
        ffn_done = sem("ffn_done")
        stored = sem("stored")

        def proj_bank(b, i):
            return scores_ps[i // 2][:, BANK * (i % 2):BANK * (i % 2) + BANK] if b == -2 else misc_ps[:, :]

        block = ctx.enter_context(nc.Block())

        def rows(eng, step):
            for b in range(-3, 1):
                step(b, b % 2, lambda off, b=b: 0 <= b + off < B)
            with eng.Fori(0, (B - 4) // 2) as i:
                step((i, 1), 1, lambda off: True)
                step((i, 2), 0, lambda off: True)
            for b in range(B - 3, B + 1):
                step(b, b % 2, lambda off, b=b: 0 <= b + off < B)

        @block.sync
        def _(sp):
            sp.dma_start(x_in[:, :, :], x_v[0, :, :, :]).then_inc(x_loaded, 16)
            sp.dma_start(ident[:, :], ident_dram).then_inc(ident_loaded, 16)
            sp.dma_start(wqkv_sb[:, :], w_qkv).then_inc(const_loaded, 16)
            sp.dma_start(wr_sb[:, :], Wr).then_inc(const_loaded, 16)
            sp.dma_start(br_sb[:, :], br.rearrange("(a e) -> a e", a=1)).then_inc(const_loaded, 16)
            sp.dma_start(cosT[:, :], cos_dram).then_inc(const_loaded, 16)
            sp.dma_start(sinT[:, :], sin_dram).then_inc(const_loaded, 16)
            sp.dma_start(w_out_sb[:, :], w_out).then_inc(const_loaded, 16)
            sp.dma_start(mask[:, :, :], mask_dram).then_inc(const_loaded, 16)
            for half in range(2):
                sp.dma_start(q_parts_dram[half, 3 * DH:3 * DH + 3, :], zeros_dram).then_inc(zeros_written, 16)
            for stack in (k_stack[0], q_stack[0]):
                sp.dma_start(stack[ROWS:128, :].rearrange("c (a n) -> c a n", a=2),
                             zeros_dram[0:1, :].unsqueeze(1).to_broadcast([128 - ROWS, 2, HALF_COLS]))\
                  .then_inc(stack_const[0], 16)
            sp.dma_start(k_stack[0][M_ROW:ROWS, :], ones_dram).then_inc(stack_const[0], 16)
            sp.wait_ge(zeros_written, 32)

            def write_parts(b, qk):
                split = value(sp, at(2, b, 2, qk))
                for half in range(2):
                    if qk == 0 and later(v := at(LOADS, b, 1, LOADS - 1)):
                        sp.wait_ge(stack_loaded[half], v)
                    if half == 0:
                        sp.wait_ge(part2_done, split)
                    sp.dma_start(parts_view((q_parts_dram, k_parts_dram)[qk], half),
                                 parts[64 * half:64 * half + 64, qk, :, :]).then_inc(parts_written[half], 16)

            def load_stack(b, off, half, par, last_use):
                free, written = value(sp, last_use), value(sp, at(32, b, off, 31))
                if later(free):
                    sp.wait_ge(scores_done, free)
                sp.wait_ge(parts_written[half], written)
                cols = slice(half * HALF_COLS, (half + 1) * HALF_COLS)
                for z0, z1 in RUNS:
                    n = z1 - z0
                    sp.dma_start(k_stack[par][DH * z0:DH * z1, cols], k_parts_dram[half, 0:DH * n, :])\
                      .then_inc(stack_loaded[half], 16)
                    q0 = DH * Q_PART[z0]
                    if n > 1:
                        sp.dma_start(q_stack[par][DH * z0:DH * z1, cols],
                                     q_parts_dram[half, q0:q0 + DH, :].unsqueeze(0)
                                     .to_broadcast([n, DH, HALF_COLS])).then_inc(stack_loaded[half], 16)
                    else:
                        sp.dma_start(q_stack[par][DH * z0:ROWS, cols], q_parts_dram[half, q0:q0 + DH + 3, :])\
                          .then_inc(stack_loaded[half], 16)

            def load_m_rows(b, off, half, par):
                sp.wait_ge(m_split, at(8, b, off, 4 * half + 3))
                for part in range(3):
                    sp.dma_start(q_stack[par][M_ROW + part:M_ROW + part + 1, half * HALF_COLS:(half + 1) * HALF_COLS]
                                 .rearrange("c (g q) -> c g q", q=KB), m_parts[:, half, part, :])\
                      .then_inc(m_rows_loaded[half], 16)

            def write_pv(half):
                sp.dma_start(pv_dram[128 * half:128 * half + 128, :], pv_sb[:, half, :]).then_inc(pv_written, 16)

            def gather(b, off):
                sp.wait_ge(pv_written, at(32, b, off, 31))
                src = pv_dram.rearrange("(a e r) n -> e a r n", e=2, r=16)
                for e, dst in enumerate((numer, denom)):
                    sp.dma_start(dst[:, :], src[e]).then_inc(gathered, 16)

            def step(b, par, has):
                if b == -1:
                    sp.wait_ge(zeroed, 4)
                    sp.dma_start(k_stack[1][M_ROW:ROWS, :], ones_dram).then_inc(stack_const[1], 16)
                if has(1):
                    load_stack(b, 1, 1, 1 - par, at(SLOTS, b, -1, 17))
                if has(3) and b != -3:
                    sp.wait_ge(xnT_ps_done, at(1, b, 2, 0))
                    sp.dma_start(x_in[:, :, :], x_v[row(b, 3), :, :, :]).then_inc(x_loaded, 16)
                if has(0):
                    load_m_rows(b, 0, 1, par)
                if has(-1):
                    sp.wait_ge(pv_copied, at(2, b, -1, 1))
                    write_pv(1)
                    gather(b, -1)
                if has(2):
                    first, second = value(sp, at(1, b, 0, 0)), value(sp, at(1, b, 2, 0))
                    split = value(sp, at(1, b, 1, 0)) if b != -2 else None
                    sp.wait_ge(const_loaded, CONSTS)
                    if later(first):
                        sp.wait_ge(ffn_done, first)
                    sp.wait_ge(expert_done, second)
                    if split is not None:
                        sp.wait_ge(w1_lo_done, split)
                    e = sp.value_load(route_idx[0:1, 0:1], min_val=0, max_val=E - 1)
                    sp.dma_start(w1_sb[:, :], W1[e, :, :]).then_inc(expert_loaded, 16)
                    sp.dma_start(w2_sb[par][:, :, :], W2[e, :, :].rearrange("(c p) d -> p c d", p=128))\
                      .then_inc(expert_loaded, 16)
                    with nc.allow_non_contiguous_dma(reason="a bias value per partition"):
                        sp.dma_start(b1_sb[par][:, :], b1[e, :].rearrange("(c p) -> p c", p=128))\
                          .then_inc(expert_loaded, 16)
                        sp.dma_start(b2_sb[par][:, :], b2[e, :].unsqueeze(0).to_broadcast([128, D]))\
                          .then_inc(expert_loaded, 16)
                if has(2):
                    for qk in range(2):
                        write_parts(b, qk)
                if has(1):
                    load_m_rows(b, 1, 0, 1 - par)
                if has(0):
                    first, second = value(sp, at(1, b, -1, 0)), value(sp, at(2, b, 0, 0))
                    if later(first):
                        sp.wait_ge(attn_done, first)
                    sp.wait_ge(pv_copied, second)
                    write_pv(0)
                if has(2):
                    load_stack(b, 2, 0, par, at(SLOTS, b, 0, 8))
                if has(-1):
                    sp.wait_ge(out_done, at(1, b, -1, 0))
                    sp.dma_start(out_v[row(b, -1), :, :, :], out_sb[:, :, :]).then_inc(stored, 16)
                if has(0):
                    if later(v := at(16, b, -1, 15)):
                        sp.wait_ge(stored, v)
                    sp.dma_start(x_res[:, :, :], x_v[row(b, 0), :, :, :]).then_inc(res_loaded, 16)

            rows(sp, step)
            sp.wait_ge(stored, 16 * B)

        @block.gpsimd
        def _(pool):
            pool.memset(minus_half[:, :], -0.5).then_inc(half_ready, 1)
            pool.wait_ge(half_ready, 1)

            def fill_pads():
                pads = [(0, 8, 0.0), (64, 0, 0.0), (0, 16, 1.0), (64, 16, 0.0), (0, 24, 0.0), (64, 24, 1.0)]
                pool.wait_ge(rstd_done, 1)
                for n in range(12):
                    first, col, fill = pads[n % 6]
                    if later(v := n):
                        pool.wait_ge(pad_ready, v)
                    pool.memset(v_pad[n // 6][first:first + 64, :, :, col:col + 8], fill).then_inc(pad_ready, 1)
                pool.wait_ge(pad_ready, 12)

            def diagonals(group, r):
                heads = slice(64 * r, 64 * r + 64)
                if group == 4:
                    return [probs[heads, 8:9, :].rearrange("k c (p n) -> k (c p) n", p=PH)[:, :, 0:KB]]
                chunks = probs[heads, 2 * group:2 * group + 2, :]
                banks = chunks.rearrange("k c (a n) -> k (c a) n", a=2)[:, :, 0:KB]
                if group < 2:
                    return [banks, chunks[:, :, 960:1024]]
                return [banks, chunks[:, :, 384:384 + KB], chunks[:, :, 832:832 + KB]]

            def mask_group(b, half, group):
                ops = GROUP_OPS[group]
                chunk = min(2 * group + 1, 8)
                exps = value(pool, at(SLOTS, b, 0, 9 * half + chunk))
                even = value(pool, at(N_MASK, b, 0, masked_after(half, group) - ops - 1))
                both = value(pool, at(N_MASK, b, 0, masked_after(half, group) - 1))
                pool.wait_ge(const_loaded, CONSTS)
                pool.wait_ge(exp_done, exps)
                for r in range(2):
                    if r == 1:
                        pool.wait_ge(const_loaded, CONSTS)
                        pool.wait_ge(masked, even)
                    for view in diagonals(group, r):
                        pattern = [[0, n] for n in view.shape[1:-1]] + [[1, KB]]
                        pool.affine_select(out=view, in_=view, compare_op=ALU.is_ge, fill=0.0, base=0,
                                           pattern=pattern, channel_multiplier=-1).then_inc(masked, 1)
                pool.wait_ge(const_loaded, CONSTS)
                pool.wait_ge(masked, both)

            def rotate(b, qk):
                pool.wait_ge(rope_done, at(4, b, 2, 2 * qk + 1))
                pool.tensor_tensor(rope_a[:, qk, :], rope_a[:, qk, :], rope_b[:, qk, :], ALU.add)\
                    .then_inc(rotated, 1)

            def rest(b, qk):
                pool.wait_ge(part0_done, at(2, b, 2, qk))
                pool.tensor_tensor(rope_b[:, qk, :], rope_a[:, qk, :], parts[:, qk, 0, :], ALU.subtract)\
                    .then_inc(rest_done, 1)

            def last_part(b, qk):
                pool.wait_ge(part1_done, at(2, b, 2, qk))
                pool.tensor_tensor(parts[:, qk, 2, :], rope_b[:, qk, :], parts[:, qk, 1, :], ALU.subtract)\
                    .then_inc(part2_done, 1)

            def step(b, par, has):
                for k in range(SLOTS):
                    if k in GROUP_SLOT and has(0):
                        mask_group(b, *GROUP_SLOT[k])
                    if k == 2 and has(2):
                        pool.wait_ge(hi_done, at(1, b, 2, 0))
                        pool.tensor_tensor(xnT_lo[par][:, :], xnT[par][:, :], xnT_hi[par][:, :], ALU.subtract)\
                            .then_inc(lo_done, 1)
                    if k == 4 and has(-1):
                        added, loaded = value(pool, at(1, b, -1, 0)), value(pool, at(16, b, -1, 15))
                        pool.wait_ge(const_loaded, CONSTS)
                        pool.wait_ge(ffn_done, added)
                        pool.wait_ge(res_loaded, loaded)
                        ffn_sum = ffn[1 - par][:, :, :]
                        pool.tensor_tensor(ffn_sum, ffn_sum, x_res[:, :, :], ALU.add).then_inc(residual_done, 1)
                    if k == 5 and has(2):
                        rotate(b, 0)
                    if k == 8 and has(2):
                        rest(b, 0)
                        if b != -2:
                            rotate(b, 1)
                    if k == 10 and has(2):
                        last_part(b, 0)
                        if b != -2:
                            rest(b, 1)
                    if k == 12 and has(2) and b != -2:
                        last_part(b, 1)
                    if k == 13 and has(3):
                        pool.wait_ge(var_done, at(1, b, 3, 0))
                        pool.tensor_tensor(rstd[:, :], var_eps[:, :], minus_half[:, :], ALU.pow)\
                            .then_inc(rstd_done, 1)
                    if k == 15 and has(2):
                        pool.wait_ge(w1_hi_done, at(1, b, 2, 0))
                        pool.tensor_tensor(w1_lo[:, :], w1_sb[:, :], w1_hi[:, :], ALU.subtract)\
                            .then_inc(w1_lo_done, 1)
                if b == -3:
                    fill_pads()
                if b == -2:
                    for n in range(4):
                        if n == 0:
                            pool.wait_ge(w1_lo_done, 1)
                        else:
                            pool.wait_ge(zeroed, n)
                        r0, r1 = ZERO_ROWS[n % 2]
                        pool.memset((q_stack[1], k_stack[1])[n // 2][r0:r1, :].bitcast(fp32), 0.0)\
                            .then_inc(zeroed, 1)
                    pool.wait_ge(zeroed, 4)

            rows(pool, step)

        @block.scalar
        def _(act):
            act.wait_ge(half_ready, 1)
            nc.scalar.activation(x_sum[:, :], minus_half[:, 0:1], ACT.Exp).then_inc(table_loaded, 1)
            act.wait_ge(table_loaded, 1)

            def exp(b, k):
                act.wait_ge(scores_done, at(SLOTS, b, 0, k))
                last = 1 if k % 9 < 4 else 4
                if later(v := at(N_PV, b, 0, last) if k >= 9 else at(N_PV, b, -1, 5 + last)):
                    act.wait_ge(pv_done, v)
                nc.scalar.activation(probs[:, k % 9, :], scores_ps[k % 2][:, :], ACT.Exp, scale=SCALE)\
                  .then_inc(exp_done, 1)

            def copy_pv(b, off, half):
                act.wait_ge(pv_done, at(N_PV, b, off, 5 * half + 4))
                nc.scalar.activation(pv_sb[:, half, :], pv_ps[:, :], ACT.Copy).then_inc(pv_copied, 1)

            def relu(b, par, c):
                act.wait_ge(ffn1_done, at(FC, b, 1, c))
                nc.scalar.activation(hT[:, c, :], misc_ps[:, :], ACT.Relu, bias=b1_sb[1 - par][:, c:c + 1])\
                  .then_inc(relu_done, 1)

            def part(b, qk, i):
                src = rope_a if i == 0 else rope_b
                act.wait_ge(rotated if i == 0 else rest_done, at(2, b, 2, qk))
                if i == 0 and qk == 0:
                    for half in range(2):
                        if later(v := at(32, b, 1, 31)):
                            act.wait_ge(parts_written[half], v)
                nc.scalar.activation(parts[:, qk, i, :], src[:, qk, :], ACT.Copy)\
                  .then_inc(part0_done if i == 0 else part1_done, 1)

            def step(b, par, has):
                for k in range(SLOTS):
                    if has(0):
                        exp(b, k)
                    if k == 0 and has(2):
                        if later(v := at(1, b, 1, 0)):
                            act.wait_ge(mean_done, v)
                        act.wait_ge(xnT_ps_done, at(1, b, 2, 0))
                        nc.scalar.activation(xnT[par][:, :], misc_ps[:, :], ACT.Identity, accum_out=x_sum[:, :])\
                          .then_inc(xnT_done, 1)
                    if k == 1 and has(2):
                        act.wait_ge(xnT_done, at(1, b, 2, 0))
                        nc.scalar.activation(xnT_hi[par][:, :], xnT[par][:, :], ACT.Copy).then_inc(hi_done, 1)
                    if k == 3 and has(-1):
                        copy_pv(b, -1, 1)
                    if k == 3 and has(1):
                        if b == -1:
                            act.wait_ge(pad_ready, 12)
                        act.wait_ge(v_ps_done, at(1, b, 1, 0))
                        for r in range(2):
                            nc.scalar.activation(
                                v_pad[1 - par][64 * r:64 * r + 64, :, :, 8 * r:8 * r + 8],
                                misc_ps[64 * r:64 * r + 64, :].rearrange("k (j p d) -> k j p d", j=NBLK, d=DH),
                                ACT.Copy).then_inc(v_done, 1)
                    if k == 7 and has(2):
                        part(b, 0, 0)
                    if k == 10 and has(2):
                        part(b, 0, 1)
                        part(b, 1, 0)
                    if k in FFN_SLOTS and has(1):
                        relu(b, par, FFN_SLOTS.index(k))
                    if k == 11 and has(0):
                        copy_pv(b, 0, 0)
                    if k == 12 and has(2):
                        part(b, 1, 1)
                    if k == 14 and has(2):
                        act.wait_ge(expert_loaded, at(64, b, 2, 63))
                        nc.scalar.activation(w1_hi[:, :], w1_sb[:, :], ACT.Copy).then_inc(w1_hi_done, 1)

            rows(act, step)

        @block.tensor
        def _(pe):
            pe.wait_ge(ident_loaded, 16)

            def slot_cols(half, r, p):
                return (half * 8 + r * PH + p) * S

            def bank_blocks(ps, bank, chunk, half, stat, mov, transposed):
                here = [(p, j, col - BANK * bank) for p, j, col in pieces(chunk) if col // BANK == bank]
                if not transposed:
                    diag = [(col + S - KB * j - KB) // KB for _, j, col in here]
                    n = len(diag)
                    step = diag[-1] - diag[0] if n == 2 else 1
                    diagonals = ps.rearrange("p (a n) -> p a n", n=KB)[:, diag[0]:diag[-1] + 1:step, :]
                    nc.tensor.matmul(diagonals, mask[:, 0, :],
                                     mask[:, 1, 0:n * KB].rearrange("k (a n) -> k a n", n=KB),
                                     start=True, stop=False, skip_group_check=True)
                for n, (p, j, col) in enumerate(here):
                    width = S - KB * j
                    stat_at = KB * (j if transposed else NBLK - 1 - j)
                    mov_at = KB * j if transposed else 0
                    for r in range(2):
                        c = slot_cols(half, r, p)
                        last = nc.tensor.matmul(ps[64 * r:64 * r + 64, col:col + width],
                                                stat[:, c + stat_at:c + stat_at + KB],
                                                mov[:, c + mov_at:c + mov_at + width],
                                                start=transposed, stop=transposed or n == len(here) - 1,
                                                skip_group_check=not transposed)
                return last

            def scores(b, par, k):
                if k % 9 == 0:
                    pe.wait_ge(m_rows_loaded[k // 9], at(48, b, 0, 47))
                if later(v := at(SLOTS, b, 0, k - 2)):
                    pe.wait_ge(exp_done, v)
                for bank in range(2):
                    last = bank_blocks(scores_ps[k % 2][:, bank * BANK:(bank + 1) * BANK], bank, k % 9, k // 9,
                                       k_stack[par], q_stack[par], True)
                last.then_inc(scores_done, 1)

            def max_scores(b, par, k):
                if k % 9 == 0:
                    pe.wait_ge(stack_loaded[k // 9], at(LOADS, b, 1, LOADS - 1))
                    if k == 0 and b in (-1, 0):
                        pe.wait_ge(stack_const[1 - par], 48 if b == -1 else 16)
                for bank in range(2):
                    if later(v := at(N_MAX, b, 1, 2 * k + bank - 2)):
                        pe.wait_ge(block_max_done, v)
                    bank_blocks(max_ps[bank][:, :], bank, k % 9, k // 9, q_stack[1 - par],
                                k_stack[1 - par], False).then_inc(max_mm_done, 1)

            def pv(b, off, par, half, i):
                blocks, group = PV_PARTS[i]
                if i == 0:
                    pe.wait_ge(v_done, at(2, b, off, 1))
                    if later(v := at(2, b, off, half - 1)):
                        pe.wait_ge(pv_copied, v)
                pe.wait_ge(masked, at(N_MASK, b, off, masked_after(half, group) - 1))
                for j in blocks:
                    for p in range(PH):
                        ch, col = PLACE[p, j]
                        last = nc.tensor.matmul(pv_ps[32 * p:32 * p + 32, KB * j:S],
                                                v_pad[par][:, j, PH * half + p, :],
                                                probs[:, ch, col:col + S - KB * j],
                                                start=(j == 0), stop=(j == 4), skip_group_check=True)
                last.then_inc(pv_done, 1)

            def transpose_max(b, off, half):
                pe.wait_ge(row_max_done, at(16, b, off, 8 * half + 7))
                for r in range(2):
                    last = nc.tensor.matmul(misc_ps[32 * r:32 * r + 32, 0:KB],
                                            row_max[:, half, :, :].rearrange("q p i -> q (p i)"),
                                            ident[:, KB * r:KB * r + KB], start=True, stop=True)
                last.then_inc(maxT_done, 1)

            def split_product(ps, w_hi, w_lo, par):
                nc.tensor.matmul(ps, w_hi, xnT_hi[par][:, :], start=True, stop=False)
                nc.tensor.matmul(ps, w_hi, xnT_lo[par][:, :], start=False, stop=False)
                return nc.tensor.matmul(ps, w_lo, xnT_hi[par][:, :], start=False, stop=True)

            def project(b, par, i, has):
                if i == 0:
                    if b == -2:
                        pe.wait_ge(w_ready, 14)
                    elif has(1):
                        pe.wait_ge(v_done, at(2, b, 1, 1))
                    else:
                        pe.wait_ge(route_done, at(1, b, 2, 0))
                    pe.wait_ge(lo_done, at(1, b, 2, 0))
                elif b != -2:
                    pe.wait_ge(rope_done, at(4, b, 2, i - 1))
                split_product(proj_bank(b, i), w_rope_hi[:, i, :], w_rope_lo[:, i, :], par).then_inc(proj_done, 1)

            def misc(b, par, k, has):
                if k == 0 and has(2):
                    if later(v := at(1, b, 0, 0)):
                        pe.wait_ge(ffn_done, v)
                    pe.wait_ge(xn_done, at(TT, b, 2, TT - 1))
                    for t in range(TT):
                        last = nc.tensor.transpose(misc_ps[:, 128 * t:128 * t + 128], x_in[:, t, :], ident[:, :])
                    last.then_inc(xnT_ps_done, 1)
                if k == 1 and has(0):
                    pe.wait_ge(xnT_done if has(2) else ffn_done, at(1, b, 2 if has(2) else 0, 0))
                    transpose_max(b, 0, 1)
                if k == 2 and b == -2:
                    pe.wait_ge(const_loaded, CONSTS)
                if k == 2 and has(2):
                    if later(v := at(8, b, 0, 5)):
                        pe.wait_ge(m_split, v)
                    else:
                        pe.wait_ge(mean_done, at(1, b, 2, 0))
                    nc.tensor.matmul(misc_ps[0:1, 0:E], x_mean[:, :], wr_sb[:, :], start=True, stop=True)\
                      .then_inc(route_ps_done, 1)
                if k == 3 and has(1):
                    if has(2):
                        pe.wait_ge(route_done, at(1, b, 2, 0))
                    elif later(v := at(8, b, 0, 5)):
                        pe.wait_ge(m_split, v)
                    for j in range(NBLK):
                        for r in range(2):
                            last = nc.tensor.matmul(
                                misc_ps[64 * r:64 * r + 64, KB * j:KB * j + KB],
                                xnT[1 - par][:, KB * j:KB * j + KB],
                                wqkv_sb[:, 2 * D:3 * D].rearrange("k (p r d) -> k p r d", r=2, d=DH)[:, :, r, :],
                                start=True, stop=True)
                    last.then_inc(v_ps_done, 1)
                if has(2):
                    for i in range(4):
                        if proj_slot(b, i) == k:
                            project(b, par, i, has)
                if k in FFN_SLOTS and has(1):
                    c = FFN_SLOTS.index(k)
                    if c == 0:
                        if has(2):
                            pe.wait_ge(rope_done, at(4, b, 2, 3))
                        else:
                            pe.wait_ge(v_done, at(2, b, 1, 1))
                        pe.wait_ge(w1_lo_done, at(1, b, 1, 0))
                    if c == 1:
                        pe.wait_ge(relu_done, at(FC, b, 1, 0))
                    if c == 2:
                        pe.wait_ge(m_split, at(8, b, 1, 1))
                    if c == 3:
                        if has(-1):
                            pe.wait_ge(out_done, at(1, b, -1, 0))
                        else:
                            pe.wait_ge(relu_done, at(FC, b, 1, 2))
                    split_product(misc_ps[:, :], w1_hi[:, 128 * c:128 * c + 128], w1_lo[:, 128 * c:128 * c + 128],
                                  1 - par).then_inc(ffn1_done, 1)
                if k == 10 and has(1):
                    pe.wait_ge(relu_done, at(FC, b, 1, 1))
                    transpose_max(b, 1, 0)
                if k == 12 and has(-1):
                    if has(1):
                        pe.wait_ge(relu_done, at(FC, b, 1, 2))
                    elif has(0):
                        pe.wait_ge(m_split, at(8, b, 0, 5))
                    else:
                        pe.wait_ge(out_done, at(1, b, -2, 0))
                    pe.wait_ge(attn_done, at(1, b, -1, 0))
                    for t in range(TT):
                        last = nc.tensor.matmul(misc_ps[:, 128 * t:128 * t + 128], numer[:, 128 * t:128 * t + 128],
                                                w_out_sb[:, :], start=True, stop=True)
                    last.then_inc(proj_out_done, 1)
                if k in (15, 16, 17) and has(1):
                    if k == 15:
                        pe.wait_ge(relu_done, at(FC, b, 1, FC - 1))
                    for t in {15: [0], 16: [1, 2], 17: [3]}[k]:
                        for c in range(FC):
                            last = nc.tensor.matmul(misc_ps[:, 128 * t:128 * t + 128],
                                                    hT[:, c, 128 * t:128 * t + 128], w2_sb[1 - par][:, c, :],
                                                    start=(c == 0), stop=(c == FC - 1))
                    if k == 17:
                        last.then_inc(ffn2_done, 1)

            def step(b, par, has):
                for k in range(SLOTS):
                    if has(0):
                        scores(b, par, k)
                    if k in PV_SLOT and has(PV_SLOT[k][0]):
                        off, half, i = PV_SLOT[k]
                        pv(b, off, par if off == 0 else 1 - par, half, i)
                    if has(1):
                        max_scores(b, par, k)
                    misc(b, par, k, has)

            rows(pe, step)

        @block.vector
        def _(dve):
            def order_weights():
                w_rope = hT[:, :, 0:D]
                dve.wait_ge(const_loaded, CONSTS)
                for qk in range(2):
                    for half in range(2):
                        src = wqkv_sb[:, qk * D + 64 * half:qk * D + 64 * half + 64]\
                            .rearrange("k (p r d) -> k d r p", r=2, d=DH)
                        plain, swapped = (w_rope[:, 2 * qk + i, 64 * half:64 * half + 64]
                                          .rearrange("k (d r p) -> k d r p", r=2, d=DH) for i in range(2))
                        nc.vector.tensor_copy(plain, src).then_inc(w_ready, 1)
                        nc.vector.tensor_copy(swapped[:, 0:4, :, :], src[:, 4:8, :, :]).then_inc(w_ready, 1)
                        nc.vector.tensor_copy(swapped[:, 4:8, :, :], src[:, 0:4, :, :]).then_inc(w_ready, 1)
                dve.wait_ge(w_ready, 12)
                nc.vector.tensor_copy(w_rope_hi[:, :, :], w_rope).then_inc(w_ready, 1)
                dve.wait_ge(w_ready, 13)
                nc.vector.tensor_tensor(w_rope_lo[:, :, :], w_rope, w_rope_hi[:, :, :], ALU.subtract)\
                  .then_inc(w_ready, 1)

            def block_maxima(b, k):
                for bank in range(2):
                    dve.wait_ge(max_mm_done, at(N_MAX, b, 1, 2 * k + bank))
                    nc.vector.tensor_reduce(block_max[:, k // 9, k % 9, 8 * bank:8 * bank + 8],
                                            max_ps[bank][:, :].rearrange("q (a c) -> q a c", c=KB),
                                            AX.X, ALU.max).then_inc(block_max_done, 1)

            def row_maxima(b, off, half):
                dve.wait_ge(block_max_done, at(N_MAX, b, off, 18 * half + 17))
                for j in range(NBLK):
                    chunk, col = PLACE[0, j]
                    n, a = NBLK - j, col // KB
                    if chunk == 8:
                        src = block_max[:, half, 8, :].rearrange("q (p a) -> q p a", p=PH)
                    else:
                        src = block_max[:, half, chunk:chunk + PH, a:a + n]
                    nc.vector.tensor_reduce(row_max[:, half, :, NBLK - 1 - j], src, AX.X, ALU.max)\
                      .then_inc(row_max_done, 1)

            def split_max(b, off, half):
                mT = misc_ps[0:64, 0:KB]
                if later(v := at(48, b, off - 1, 47)):
                    dve.wait_ge(m_rows_loaded[half], v)
                dve.wait_ge(maxT_done, at(2, b, off, half))
                nc.vector.tensor_scalar(m_parts[:, half, 0, :], mT, -1.0, None, ALU.mult).then_inc(m_split, 1)
                dve.wait_ge(m_split, at(8, b, off, 4 * half))
                nc.vector.scalar_tensor_tensor(out=m_rest[:, :], in0=mT, scalar=-1.0, in1=m_parts[:, half, 0, :],
                                               op0=ALU.mult, op1=ALU.subtract).then_inc(m_split, 1)
                dve.wait_ge(m_split, at(8, b, off, 4 * half + 1))
                nc.vector.tensor_copy(m_parts[:, half, 1, :], m_rest[:, :]).then_inc(m_split, 1)
                dve.wait_ge(m_split, at(8, b, off, 4 * half + 2))
                nc.vector.tensor_tensor(m_parts[:, half, 2, :], m_rest[:, :], m_parts[:, half, 1, :],
                                        ALU.subtract).then_inc(m_split, 1)

            def rope(b, i):
                dve.wait_ge(proj_done, at(4, b, 2, i))
                dst, table = ((rope_a, cosT), (rope_b, sinT))[i % 2]
                if i % 2:
                    if later(v := at(2, b, 1, i // 2)):
                        dve.wait_ge(part2_done, v)
                nc.vector.tensor_tensor(dst[:, i // 2, :], proj_bank(b, i), table[:, :], ALU.mult)\
                  .then_inc(rope_done, 1)

            def first_k_parts():
                k, k_rest = rope_a[:, 1, :], rope_b[:, 1, :]
                dve.wait_ge(rope_done, 4)
                dve.wait_ge(rotated, 1)
                nc.vector.tensor_tensor(k, k, k_rest, ALU.add).then_inc(rotated, 1)
                dve.wait_ge(part0_done, 2)
                dve.wait_ge(rest_done, 1)
                nc.vector.tensor_tensor(k_rest, k, parts[:, 1, 0, :], ALU.subtract).then_inc(rest_done, 1)
                dve.wait_ge(part1_done, 2)
                dve.wait_ge(part2_done, 1)
                nc.vector.tensor_tensor(parts[:, 1, 2, :], k_rest, parts[:, 1, 1, :], ALU.subtract)\
                  .then_inc(part2_done, 1)

            def router(b):
                dve.wait_ge(route_ps_done, at(1, b, 2, 0))
                nc.vector.tensor_tensor(route[:, :], misc_ps[0:1, 0:E], br_sb[:, :], ALU.add)\
                  .then_inc(route_done, 1)
                done = value(dve, at(1, b, 2, 0))
                dve.wait_ge(const_loaded, CONSTS)
                dve.wait_ge(route_done, done)
                nc.vector.max(route_max[:, :], route[:, :]).then_inc(top_done, 1)
                loaded = value(dve, at(64, b, 1, 63))
                dve.wait_ge(const_loaded, CONSTS)
                dve.wait_ge(top_done, done)
                if later(v := loaded):
                    dve.wait_ge(expert_loaded, v)
                nc.vector.max_index(route_idx[:, :], route_max[:, :], route[:, :]).then_inc(expert_done, 1)

            def reciprocals(b, quarter):
                cols = slice(128 * quarter, 128 * quarter + 128)
                if quarter == 0:
                    dve.wait_ge(gathered, at(32, b, -1, 31))
                nc.vector.reciprocal(denom[:, cols], denom[:, cols]).then_inc(recip_done, 1)

            def normalise(b):
                dve.wait_ge(recip_done, at(4, b, -1, 3))
                nc.vector.tensor_tensor(numer[:, :], numer[:, :], denom[:, :], ALU.mult).then_inc(attn_done, 1)

            def ln_stats(b):
                dve.wait_ge(x_loaded, at(16, b, 3, 15))
                for t in range(TT):
                    nc.vector.bn_stats(stats[:, t, :], x_in[:, t, :]).then_inc(stats_done, 1)
                for t in range(TT):
                    done = value(dve, at(TT, b, 3, t))
                    dve.wait_ge(x_loaded, 16)
                    dve.wait_ge(stats_done, done)
                    nc.vector.bn_aggr(mean_var[:, t, :], stats[:, t, :]).then_inc(aggr_done, 1)
                dve.wait_ge(aggr_done, at(TT, b, 3, TT - 1))
                nc.vector.tensor_scalar(var_eps[:, :], mean_var[:, :, 1], EPS, None, ALU.add).then_inc(var_done, 1)

            def ln_apply(b):
                dve.wait_ge(rstd_done, at(1, b, 3, 0))
                for t in range(TT):
                    nc.vector.tensor_scalar(x_in[:, t, :], x_in[:, t, :], mean_var[:, t, 0:1], rstd[:, t:t + 1],
                                            ALU.subtract, ALU.mult).then_inc(xn_done, 1)

            def step(b, par, has):
                for k in range(SLOTS):
                    if k == 0 and has(0):
                        row_maxima(b, 0, 1)
                    if has(1):
                        block_maxima(b, k)
                    if k == 0 and has(2):
                        dve.wait_ge(xnT_done, at(1, b, 2, 0))
                        nc.vector.tensor_scalar(x_mean[:, :], x_sum[:, :], 1.0 / S, None, ALU.mult)\
                          .then_inc(mean_done, 1)
                    if k == 1 and has(0):
                        split_max(b, 0, 1)
                    if k == 2 and has(2):
                        router(b)
                    if has(2):
                        for i in range(4):
                            if proj_slot(b, i) == k:
                                rope(b, i)
                    if k == 8 and b == -2:
                        first_k_parts()
                    if k == 9 and has(1):
                        row_maxima(b, 1, 0)
                    if k == 10 and has(1):
                        split_max(b, 1, 0)
                    if has(-1):
                        for quarter in [n for n in range(4) if RECIP_SLOTS[n] == k]:
                            reciprocals(b, quarter)
                    if k == 11 and has(-1):
                        normalise(b)
                    if k == 12 and has(-1):
                        dve.wait_ge(proj_out_done, at(1, b, -1, 0))
                        dve.wait_ge(residual_done, at(1, b, -1, 0))
                        nc.vector.tensor_tensor(out_sb[:, :, :], misc_ps[:, :].rearrange("p (t d) -> p t d", d=D),
                                                ffn[1 - par][:, :, :], ALU.add).then_inc(out_done, 1)
                    if k == 13 and has(3):
                        ln_stats(b)
                    if k == 15 and has(3):
                        ln_apply(b)
                    if k == 15 and b == -3:
                        order_weights()
                    if k == 17 and has(1):
                        dve.wait_ge(ffn2_done, at(1, b, 1, 0))
                        nc.vector.tensor_tensor(ffn[1 - par][:, :, :],
                                                misc_ps[:, :].rearrange("p (t d) -> p t d", d=D),
                                                b2_sb[1 - par][:, :].unsqueeze(1).to_broadcast([128, TT, D]),
                                                ALU.add).then_inc(ffn_done, 1)

            rows(dve, step)


_INS = ['L0_attn_x', 'L0_attn_w_qkv', 'L0_attn_w_out', 'L0_ffn_Wr', 'L0_ffn_br', 'L0_ffn_W1', 'L0_ffn_b1',
        'L0_ffn_W2', 'L0_ffn_b2']
_OUTS = [((16, 512, 128), 'float32')]


def _constants():
    import numpy as np
    from concourse import mybir
    bf16 = mybir.dt.np(mybir.dt.bfloat16)
    S, DH, KB, MASKED = 512, 8, 64, -1e30
    ident = np.eye(128, dtype=np.float32)
    inv_freq = (1.0 / np.float32(10000.0) ** (np.arange(0, DH, 2, dtype=np.float32) / DH)).astype(np.float32)
    freqs = np.arange(S, dtype=np.float32)[:, None] * inv_freq[None, :]
    cos, sin = np.cos(freqs).astype(np.float32), np.sin(freqs).astype(np.float32)
    d = (np.arange(128) % 64) // 8
    cosT = np.ascontiguousarray(cos[:, d % 4].T)
    sinT = np.ascontiguousarray(sin[:, d % 4].T * np.where(d < 4, -1, 1)[:, None].astype(np.float32))
    n, m = np.arange(128)[:, None], np.arange(128)[None, :] % KB
    mask = np.stack([np.where(n > m, MASKED, 0.0), n == m], axis=1)
    mask[KB:] = 0.0
    return {"ident": ident, "cos": cosT, "sin": sinT, "mask": mask.astype(bf16),
            "ones": np.ones((3, 16 * S), bf16), "zeros": np.zeros((3, 8 * S), bf16)}


def kernel(**inputs):
    import numpy as _np
    import concourse.bacc as _bacc
    from concourse import mybir as _mybir
    from concourse.bass_utils import run_bass_kernel_spmd as _run

    nc = _bacc.Bacc("TRN2", target_bir_lowering=False, num_devices=1)
    arrays, args = {}, []
    named = {name: inputs[name] for name in _INS} | _constants()
    for name, a in named.items():
        a = _np.ascontiguousarray(a)
        arrays[f"in_{name}_dram"] = a
        args.append(nc.dram_tensor(f"in_{name}_dram", a.shape, _mybir.dt.from_np(a.dtype), kind="ExternalInput").ap())
    for i, (shape, dtype) in enumerate(_OUTS):
        dt = _mybir.dt.from_np(_np.dtype(dtype))
        args.append(nc.dram_tensor(f"out_{i}_dram", shape, dt, kind="ExternalOutput").ap())
    out = args.pop()
    for name, rows in (("q_parts_dram", 27), ("k_parts_dram", 24)):
        args.append(nc.dram_tensor(name, (2, rows, 4096), _mybir.dt.bfloat16, kind="Internal").ap())
    args.append(nc.dram_tensor("pv_dram", (256, 512), _mybir.dt.float32, kind="Internal").ap())
    layernorm_attention_moe_kernel(nc, *args, out)
    r = _run(nc, [arrays], core_ids=[0])
    got = tuple(r.results[0][f"out_{i}_dram"] for i in range(len(_OUTS)))
    return got[0]
```
